# Optimizing a Trainium2 kernel written in Bass

```python
import numpy as np
import jax
import jax.numpy as jnp

def _softmax(x, axis=-1):
    return jax.nn.softmax(x, axis=axis)

def _gelu(x):
    return jax.nn.gelu(x, approximate=True)

def _silu(x):
    return jax.nn.silu(x)

def _sigmoid(x):
    return jax.nn.sigmoid(x)

def _layernorm(x, axis=-1, eps=1e-05):
    m = jnp.mean(x, axis=axis, keepdims=True)
    v = jnp.var(x, axis=axis, keepdims=True)
    return (x - m) / jnp.sqrt(v + eps)

def _scatter_add(tgt, idx, src, axis=0):
    return tgt.at[idx].add(src)

def _segment_sum(src, seg, n):
    return jax.ops.segment_sum(src, seg, n)
kernel_name = 'mk_adaln_ffn_d1_seqx_r8_98e348'

def setup_inputs(seed: int=0):
    np.random.seed(seed)
    _w = jnp.asarray

    def _rec_inputs():
        import jax
        import jax.numpy as jnp
        _rk = jax.random.key(seed)
        x = -7.109e-05 + 0.9999 * jax.random.normal(jax.random.fold_in(_rk, 1), (128, 32, 256), jnp.float32)
        _lenS = 32 - jax.random.randint(jax.random.fold_in(_rk, 7), (128,), 0, max(1, 32 // 4) + 1, jnp.int32)
        _lenS2 = 32 - jax.random.randint(jax.random.fold_in(_rk, 8), (128,), 0, max(1, 32 // 4) + 1, jnp.int32)
        itok_B_1_198 = jax.random.randint(jax.random.fold_in(_rk, 11), (128,), 1, 199, jnp.int32)
        return (x, itok_B_1_198)
    x, itok_B_1_198 = _rec_inputs()

    def _L0_cond_setup():
        import jax, jax.numpy as jnp
        import numpy as np
        B, C, T = (128, 32, 256)
        S, D = (200, 32)
        key = jax.random.key(seed)
        k1, k2, k3 = jax.random.split(key, 3)
        x = jax.random.normal(k1, (B, C, T), dtype=jnp.float32)
        conditions = jax.random.randint(k2, (B,), 0, S, dtype=jnp.int64)
        weights = jax.random.normal(k3, (S, C, D), dtype=jnp.float32) / jnp.sqrt(jnp.float32(C))
        return {'x': x, 'conditions': conditions, 'weights': weights}
    _L0_cond_all = _L0_cond_setup()
    _L0_cond_in = {k: v for k, v in _L0_cond_all.items() if k in ('weights',)}
    del _L0_cond_all

    def _L0_ffn_setup():
        import jax, jax.numpy as jnp
        import numpy as np
        H, LAT, INTER, E, G, TOPK_G, TOP_K = (256, 128, 128, 32, 4, 2, 8)
        SHARED_INTER = 512
        ROUTED_SCALE = 2.5
        B, S = (2, 128)

        def relu2(x):
            return jnp.square(jax.nn.relu(x))
        key = jax.random.key(seed)
        ks = jax.random.split(key, 9)
        w = 0.02
        return {'hidden_states': jax.random.normal(ks[0], (B, S, H), jnp.float32), 'gate_w': jax.random.normal(ks[1], (E, H), jnp.float32) * w, 'gate_bias': jax.random.normal(ks[2], (E,), jnp.float32) * w, 'fc1_w': jax.random.normal(ks[3], (LAT, H), jnp.float32) * w, 'fc2_w': jax.random.normal(ks[4], (H, LAT), jnp.float32) * w, 'w1': jax.random.normal(ks[5], (E, INTER, LAT), jnp.float32) * w, 'w2': jax.random.normal(ks[6], (E, LAT, INTER), jnp.float32) * w, 'shared_up_w': jax.random.normal(ks[7], (SHARED_INTER, H), jnp.float32) * w, 'shared_down_w': jax.random.normal(ks[8], (H, SHARED_INTER), jnp.float32) * w}
    _L0_ffn_all = _L0_ffn_setup()
    _L0_ffn_in = {k: v for k, v in _L0_ffn_all.items() if k in ('gate_w', 'gate_bias', 'fc1_w', 'fc2_w', 'w1', 'w2', 'shared_up_w', 'shared_down_w')}
    del _L0_ffn_all
    return {'x': x, 'itok_B_1_198': itok_B_1_198, 'L0_cond_weights': _L0_cond_in['weights'], 'L0_ffn_gate_w': _L0_ffn_in['gate_w'], 'L0_ffn_gate_bias': _L0_ffn_in['gate_bias'], 'L0_ffn_fc1_w': _L0_ffn_in['fc1_w'], 'L0_ffn_fc2_w': _L0_ffn_in['fc2_w'], 'L0_ffn_w1': _L0_ffn_in['w1'], 'L0_ffn_w2': _L0_ffn_in['w2'], 'L0_ffn_shared_up_w': _L0_ffn_in['shared_up_w'], 'L0_ffn_shared_down_w': _L0_ffn_in['shared_down_w']}

def reference(x, itok_B_1_198, L0_cond_weights, L0_ffn_gate_w, L0_ffn_gate_bias, L0_ffn_fc1_w, L0_ffn_fc2_w, L0_ffn_w1, L0_ffn_w2, L0_ffn_shared_up_w, L0_ffn_shared_down_w):
    import jax
    import jax.numpy as jnp

    def _L0_cond_ref(x, conditions, weights):
        import jax, jax.numpy as jnp
        import numpy as np
        B, C, T = (128, 32, 256)
        S, D = (200, 32)
        w = weights[conditions]
        return jnp.einsum('bct,bcd->bdt', x, w)

    def _L0_ffn_ref(hidden_states, gate_w, gate_bias, fc1_w, fc2_w, w1, w2, shared_up_w, shared_down_w):
        import jax, jax.numpy as jnp
        import numpy as np
        H, LAT, INTER, E, G, TOPK_G, TOP_K = (256, 128, 128, 32, 4, 2, 8)
        SHARED_INTER = 512
        ROUTED_SCALE = 2.5
        B, S = (2, 128)

        def relu2(x):
            return jnp.square(jax.nn.relu(x))
        orig_shape = hidden_states.shape
        x = hidden_states.reshape(-1, H)
        T = x.shape[0]
        logits = jnp.einsum('th,eh->te', x.astype(jnp.float32), gate_w)
        scores = jax.nn.sigmoid(logits)
        sb = scores + gate_bias
        grp = sb.reshape(T, G, E // G)
        group_scores = jax.lax.top_k(grp, 2)[0].sum(-1)
        _, gidx = jax.lax.top_k(group_scores, TOPK_G)
        gmask = jax.nn.one_hot(gidx, G, dtype=sb.dtype).sum(1)
        masked = jnp.where(gmask[:, :, None] > 0, grp, -jnp.inf).reshape(T, E)
        _, topi = jax.lax.top_k(masked, TOP_K)
        wsel = jnp.take_along_axis(scores, topi, axis=1)
        wsel = wsel / wsel.sum(-1, keepdims=True) * ROUTED_SCALE
        cw = jnp.zeros((T, E), jnp.float32).at[jnp.arange(T)[:, None], topi].add(wsel)
        x_lat = x @ fc1_w.T
        h = relu2(jnp.einsum('tl,eil->eti', x_lat, w1))
        h = h * cw.T[:, :, None]
        y_lat = jnp.einsum('eti,eli->tl', h, w2)
        routed = y_lat @ fc2_w.T
        shared = relu2(x @ shared_up_w.T) @ shared_down_w.T
        return (shared + routed).reshape(orig_shape)
    x = x + _L0_ffn_ref(_L0_cond_ref(x, itok_B_1_198, L0_cond_weights), L0_ffn_gate_w, L0_ffn_gate_bias, L0_ffn_fc1_w, L0_ffn_fc2_w, L0_ffn_w1, L0_ffn_w2, L0_ffn_shared_up_w, L0_ffn_shared_down_w)
    return x

_drawn_inputs = setup_inputs


def setup_inputs(seed=0):
    import zlib

    import numpy as np

    out = dict(_drawn_inputs(seed))
    spreads = {}
    factors = {'L0_ffn_gate_w': 8.0,
     'L0_ffn_gate_bias': 8.0,
     'L0_ffn_fc1_w': 8.0,
     'L0_ffn_fc2_w': 8.0,
     'L0_ffn_w1': 8.0,
     'L0_ffn_w2': 8.0,
     'L0_ffn_shared_up_w': 8.0,
     'L0_ffn_shared_down_w': 8.0}
    for name, (base, spread) in spreads.items():
        noise = np.random.default_rng([zlib.crc32(name.encode()), seed]).standard_normal(out[name].shape)
        drawn = base * np.exp(spread * noise) if base else spread * noise
        out[name] = jnp.asarray(drawn.astype(out[name].dtype))
    for name, factor in factors.items():
        out[name] = (out[name] * factor).astype(out[name].dtype)
    return out
```

```python
from contextlib import ExitStack

import concourse.bass as bass
from concourse import mybir

B, C, H = 128, 32, 256
STATES = 200
EXPERTS, LAT, INTER = 32, 128, 128
GROUPS, TOP_GROUPS, TOP_K = 4, 2, 8
GROUP_SIZE = EXPERTS // GROUPS
SHARED = 512
ROUTED_SCALE = 2.5
P = 128
TOKENS = B * C
PASSES = 2
PASS_TOKENS = TOKENS // PASSES
BANK = 512
BLOCKS = PASS_TOKENS // BANK
TILES = PASS_TOKENS // P
BT = TILES // BLOCKS
BATCH_TILE = P // C
HALVES = H // P
UNIT = 2 * BANK
SHARED_CHUNKS = SHARED // P
SHARED_UNITS = BLOCKS * 2
TOKEN_HALVES = PASS_TOKENS // UNIT
EXPERT_UNITS = EXPERTS * TOKEN_HALVES
UNITS = SHARED_UNITS + EXPERT_UNITS
W_CHUNK = 4
W_CHUNKS = EXPERTS // W_CHUNK
SMALL_CHUNKS = 3
SMALL_SPLITS = 4
SPLITS = SMALL_SPLITS + W_CHUNKS
BIG = 1e38
TAKEN = -3e38
TINY = 1e-30
GATE_STEPS = 56
DMA = 16

UP0 = 0
DOWN0 = UP0 + HALVES * SHARED
FC1_0 = DOWN0 + SHARED_CHUNKS * H
FC2_0 = FC1_0 + HALVES * LAT
GATE0 = FC2_0 + H
SMALL = GATE0 + HALVES * P


def adaln_ffn(nc, x, cond, cond_w, gate_w, gate_b, fc1_w, fc2_w, w1, w2, up_w, down_w, out):
    f32, f32r, i32 = mybir.dt.float32, mybir.dt.float32r, mybir.dt.int32
    ALU, ACT, AX = mybir.AluOpType, mybir.ActivationFunctionType, mybir.AxisListType

    x_rows = x.rearrange("b c h -> (b c) h").rearrange("(n p) h -> p n h", p=P)
    out_rows = out.rearrange("b c h -> (b c) h").rearrange("(n p) h -> p n h", p=P)

    w_split = nc.dram_tensor("w_split", (EXPERTS, P, 2, 2, P), f32).ap()
    cond_dram = nc.dram_tensor("cond_dram", (B, C, C), f32).ap()
    s_dram = nc.dram_tensor("s_dram", (EXPERTS, PASS_TOKENS), f32).ap()

    with ExitStack() as ctx:
        def sb(name, shape, dt=f32):
            return ctx.enter_context(nc.sbuf_tensor(name, shape, dt))

        def sem(name):
            return ctx.enter_context(nc.semaphore(name))

        def sems(name, n):
            return [sem(f"{name}{i}") for i in range(n)]

        x_in = sb("x_in", [P, TILES, H])
        x_res = sb("x_res", [P, TILES, H])
        cond_bd = sb("cond_bd", [P, TILES, P])
        cond_sb = sb("cond_sb", [B, 1], i32)
        cond_rows = sb("cond_rows", [B, C * C])
        xc_hi = sb("xc_hi", [P, HALVES, PASS_TOKENS], f32r)
        xc_lo = sb("xc_lo", [P, HALVES, PASS_TOKENS], f32r)
        lat_hi = sb("lat_hi", [P, PASS_TOKENS], f32r)
        lat_lo = sb("lat_lo", [P, PASS_TOKENS], f32r)
        small_hi = sb("small_hi", [P, SMALL], f32r)
        small_lo = sb("small_lo", [P, SMALL], f32r)
        w1_ring = sb("w1_ring", [P, 2, 2, P], f32r)
        w2_ring = sb("w2_ring", [P, 2, 2, P], f32r)
        scale_ring = sb("scale_ring", [P, 4, UNIT])
        scaled = sb("scaled", [P, 2, UNIT])
        act_full = sb("act_full", [P, 2, UNIT])
        act_hi = sb("act_hi", [P, 2, UNIT], f32r)
        act_lo = sb("act_lo", [P, 2, UNIT], f32r)
        s_t = sb("s_t", [P, BANK])
        ident = sb("ident", [P, P])
        bias_sb = sb("bias_sb", [P, EXPERTS])
        before = sb("before", [P, GROUPS, GROUPS])
        scores_t = sb("scores_t", [EXPERTS, PASS_TOKENS])
        scores = sb("scores", [P, TILES, EXPERTS])
        biased = sb("biased", [P, TILES, EXPERTS])
        work = sb("work", [P, TILES, EXPERTS])
        masked = sb("masked", [P, TILES, EXPERTS])
        left = sb("left", [P, TILES, EXPERTS])
        cw = sb("cw", [P, TILES, EXPERTS])
        root = sb("root", [P, TILES, EXPERTS])
        s_tok = sb("s_tok", [P, TILES, EXPERTS])
        top8 = sb("top8", [P, TILES, 8])
        first = sb("first", [P, TILES, GROUPS])
        count = sb("count", [P, TILES, GROUPS])
        second = sb("second", [P, TILES, GROUPS])
        group_score = sb("group_score", [P, TILES, GROUPS])
        group_gt = sb("group_gt", [P, TILES, GROUPS, GROUPS])
        group_eq = sb("group_eq", [P, TILES, GROUPS, GROUPS])
        total = sb("total", [P, TILES])

        raw_up = scaled[:, 0, :].rearrange("p (k h) -> p k h", h=H)
        raw_down = scaled[:, 1, :].rearrange("p (a m) -> p a m", m=SHARED)
        raw_fc1 = act_full[:, 0, 0:H]
        raw_fc2 = act_full[:, 0, H:2 * H].rearrange("p (a l) -> p a l", l=LAT)
        raw_gate = act_full[0:EXPERTS, 0, 2 * H:3 * H]
        raw_experts = x_res[:, :, :].rearrange("p (s c) h -> p s (c h)", s=4)\
            .rearrange("p s (w e i) -> p s w e i", w=2, e=W_CHUNK)

        h_banks = ctx.enter_context(nc.psum_tensor("h_banks", [P, 2, UNIT], f32))
        y_banks = ctx.enter_context(nc.psum_tensor("y_banks", [P, 2, UNIT], f32))

        x_loaded = sems("x_loaded", BLOCKS)
        cond_idx_loaded = sem("cond_idx_loaded")
        bias_loaded = sem("bias_loaded")
        small_loaded = sem("small_loaded")
        raw_loaded = sems("raw_loaded", 4)
        w_stored = sems("w_stored", 2)
        cond_gathered = sem("cond_gathered")
        cond_stored = sem("cond_stored")
        cond_loaded = sem("cond_loaded")
        s_stored = sem("s_stored")
        w1_loaded = sems("w1_loaded", 2)
        w2_loaded = sems("w2_loaded", 2)
        scale_loaded = sems("scale_loaded", 4)
        out_stored = sems("out_stored", BLOCKS)
        const_step = sem("const_step")
        consts_ready = sem("consts_ready")
        cond_zeroed = sem("cond_zeroed")
        gate_zeroed = sem("gate_zeroed")
        wt_ready = sem("wt_ready")
        xc_ready = sem("xc_ready")
        logits_ready = sem("logits_ready")
        lat_ready = sem("lat_ready")
        h_ready = sem("h_ready")
        down_done = sem("down_done")
        scores_transposed = sem("scores_transposed")
        s_t_ready = sem("s_t_ready")
        experts_done = sem("experts_done")
        fc2_done = sem("fc2_done")
        wt_hi = sem("wt_hi")
        xc_hi_ready = sem("xc_hi_ready")
        lat_hi_ready = sem("lat_hi_ready")
        scores_t_ready = sem("scores_t_ready")
        scores_ready = sem("scores_ready")
        root_ready = sem("root_ready")
        relu_ready = sem("relu_ready")
        act_hi_ready = sem("act_hi_ready")
        act_full_ready = sem("act_full_ready")
        s_t_copied = sem("s_t_copied")
        y_hi_ready = sem("y_hi_ready")
        wt_lo = sem("wt_lo")
        xc_lo_ready = sem("xc_lo_ready")
        lat_lo_ready = sem("lat_lo_ready")
        gate_step = sem("gate_step")
        cw_ready = sem("cw_ready")
        s_ready = sem("s_ready")
        scaled_ready = sem("scaled_ready")
        act_lo_ready = sem("act_lo_ready")
        shared_added = sem("shared_added")
        y_lo_ready = sem("y_lo_ready")
        routed_added = sem("routed_added")

        block = ctx.enter_context(nc.Block())

        def three(w_hi, w_lo, v_hi, v_lo):
            return ((w_hi, v_hi), (w_lo, v_hi), (w_hi, v_lo))

        @block.sync
        def _(sp):
            sp.dma_start(raw_up, up_w.rearrange("(k p) h -> p k h", p=P)).then_inc(small_loaded, DMA)
            sp.dma_start(raw_down, down_w.rearrange("(a p) m -> p a m", p=P)).then_inc(small_loaded, DMA)
            sp.dma_start(raw_fc1, fc1_w).then_inc(small_loaded, DMA)
            sp.dma_start(raw_fc2, fc2_w.rearrange("(a p) l -> p a l", p=P)).then_inc(small_loaded, DMA)
            sp.dma_start(raw_gate, gate_w).then_inc(small_loaded, DMA)

            def load_raw(c):
                e = W_CHUNK * c
                for w, src in enumerate((w1, w2)):
                    sp.dma_start(raw_experts[:, c % 4, w], src[e:e + W_CHUNK].rearrange("e p i -> p e i"))\
                        .then_inc(raw_loaded[c % 4], DMA)

            def store_split(c):
                dst = w_split[W_CHUNK * c:W_CHUNK * (c + 1)].rearrange("e p w s i -> s w p e i")
                for part, (ready, buf) in enumerate(((wt_hi, act_hi), (wt_lo, act_lo))):
                    sp.wait_ge(ready, SMALL_SPLITS + c + 1)
                    for w in range(2):
                        src = buf[:, c % 2, w * BANK:(w + 1) * BANK].bitcast(f32)
                        sp.dma_start(dst[part, w], src.rearrange("p (e i) -> p e i", e=W_CHUNK))\
                            .then_inc(w_stored[c % 2], DMA)

            for c in range(4):
                load_raw(c)
            for c in range(W_CHUNKS):
                store_split(c)
                if c + 4 < W_CHUNKS:
                    sp.wait_ge(wt_ready, SMALL_CHUNKS + c + 1)
                    load_raw(c + 4)
            for s in range(2):
                sp.wait_ge(w_stored[s], 4 * DMA * (W_CHUNKS // 2))

            def load_w(ring, loaded, w, slot, e):
                sp.dma_start(ring[:, slot].bitcast(f32),
                             w_split[bass.ds(e, 1)].rearrange("e p w s i -> p (e w) s i")[:, w])\
                    .then_inc(loaded[slot], DMA)

            def load_scale(slot, e, half):
                src = s_dram[bass.ds(e, 1), half * UNIT:(half + 1) * UNIT]
                sp.dma_start(scale_ring[:, slot, :], src.to_broadcast([P, UNIT]))\
                    .then_inc(scale_loaded[slot], DMA)

            with sp.Fori(0, PASSES) as p:
                experts_before = sp.snap(p * EXPERT_UNITS)
                sp.wait_ge(experts_done, experts_before)
                for slot in range(2):
                    load_w(w1_ring, w1_loaded, 0, slot, slot)
                    load_w(w2_ring, w2_loaded, 1, slot, slot)
                sp.wait_ge(s_t_copied, p + 1)
                for j in range(BT):
                    sp.dma_start(
                        s_dram.rearrange("e (b j t) -> j e b t", b=BLOCKS, j=BT)[j],
                        s_t[EXPERTS * j:EXPERTS * (j + 1), :].rearrange("e (b t) -> e b t", b=BLOCKS),
                    ).then_inc(s_stored, DMA)
                sp.wait_ge(s_stored, (p + 1) * BT * DMA)
                for slot in range(4):
                    load_scale(slot, slot // 2, slot % 2)
                base = sp.snap(p * UNITS + SHARED_UNITS)
                with sp.Fori(0, EXPERTS // 2 - 1) as i:
                    for k in range(2):
                        done = 4 * i + 2 * k
                        sp.wait_ge(scaled_ready, experts_before + done + 1)
                        load_scale(2 * k, 2 * i + (k + 2), 0)
                        sp.wait_ge(h_ready, base + done + 2)
                        load_w(w1_ring, w1_loaded, 0, k, 2 * i + (k + 2))
                        sp.wait_ge(scaled_ready, experts_before + done + 2)
                        load_scale(2 * k + 1, 2 * i + (k + 2), 1)
                        sp.wait_ge(experts_done, experts_before + done + 2)
                        load_w(w2_ring, w2_loaded, 1, k, 2 * i + (k + 2))
                for q in range(BLOCKS):
                    sp.wait_ge(routed_added, p * BLOCKS + q + 1)
                    sp.dma_start(out_rows[:, bass.ds(p * TILES + BT * q, BT), :],
                                 x_res[:, BT * q:BT * (q + 1), :]).then_inc(out_stored[q], DMA)
            for q in range(BLOCKS):
                sp.wait_ge(out_stored[q], PASSES * DMA)

        @block.gpsimd
        def _(pool):
            pool.dma_start(cond_sb[:, :], cond.rearrange("(b a) -> b a", a=1)).then_inc(cond_idx_loaded, DMA)
            pool.dma_start(bias_sb[:, :], gate_b.rearrange("(a e) -> a e", a=1).to_broadcast([P, EXPERTS]))\
                .then_inc(bias_loaded, DMA)
            pool.memset(ident[:, :], 0.0).then_inc(const_step, 1)
            pool.memset(before[:, :, :], 0.0).then_inc(const_step, 1)
            pool.wait_ge(const_step, 2)
            pool.affine_select(out=ident[:, :], in_=ident[:, :], compare_op=ALU.not_equal, fill=1.0, base=0,
                               pattern=[[-1, P]], channel_multiplier=1).then_inc(consts_ready, 1)
            pool.affine_select(out=before[:, :, :], in_=before[:, :, :], compare_op=ALU.is_ge, fill=1.0, base=0,
                               pattern=[[-1, GROUPS], [1, GROUPS]], channel_multiplier=0).then_inc(consts_ready, 1)
            pool.memset(small_hi[:, GATE0:SMALL].bitcast(f32), 0.0).then_inc(gate_zeroed, 1)
            pool.memset(small_lo[:, GATE0:SMALL].bitcast(f32), 0.0).then_inc(gate_zeroed, 1)
            pool.memset(cond_bd[:, :, :], 0.0).then_inc(cond_zeroed, 1)
            pool.wait_ge(cond_idx_loaded, DMA)
            pool.indirect_dma_start(
                cond_rows[:, :], None, cond_w.rearrange("s c d -> s (c d)"),
                bass.IndirectOffsetOnAxis(ap=cond_sb[:, 0:1], axis=0)).then_inc(cond_gathered, DMA)
            for b in range(BLOCKS):
                pool.dma_start(x_in[:, BT * b:BT * (b + 1), :], x_rows[:, BT * b:BT * (b + 1), :])\
                    .then_inc(x_loaded[b], DMA)
            pool.wait_ge(cond_gathered, DMA)
            pool.dma_start(cond_dram.rearrange("b c d -> b (c d)"), cond_rows[:, :]).then_inc(cond_stored, DMA)

            def load_cond(p):
                for j in range(BATCH_TILE):
                    pool.dma_start(
                        cond_bd[C * j:C * (j + 1), :, C * j:C * (j + 1)],
                        cond_dram[bass.ds(p * TILES * BATCH_TILE, TILES * BATCH_TILE)]
                        .rearrange("(g j) c d -> j c g d", j=BATCH_TILE)[j],
                    ).then_inc(cond_loaded, DMA)

            pool.wait_ge(cond_zeroed, 1)
            pool.wait_ge(cond_stored, DMA)
            load_cond(0)
            with pool.Fori(0, PASSES - 1) as p:
                pool.wait_ge(xc_ready, (p + 1) * BLOCKS)
                load_cond(p + 1)
                for b in range(BLOCKS):
                    pool.wait_ge(shared_added, p * BLOCKS + b + 1)
                    pool.dma_start(x_in[:, BT * b:BT * (b + 1), :],
                                   x_rows[:, bass.ds((p + 1) * TILES + BT * b, BT), :])\
                        .then_inc(x_loaded[b], DMA)

        @block.tensor
        def _(pe):
            def transpose_chunk(jobs):
                for dst, src, n in jobs:
                    last = pe.transpose(dst, src, ident[0:n, 0:n])
                last.then_inc(wt_ready, 1)

            pe.wait_ge(consts_ready, 1)
            pe.wait_ge(small_loaded, 5 * DMA)
            transpose_chunk([(h_banks[:, 0, a * SHARED + k * P:a * SHARED + (k + 1) * P],
                              raw_up[:, k, a * P:(a + 1) * P], P)
                             for a in range(HALVES) for k in range(SHARED_CHUNKS)])
            transpose_chunk([(h_banks[:, 1, k * H + a * P:k * H + (a + 1) * P],
                              raw_down[:, a, k * P:(k + 1) * P], P)
                             for k in range(SHARED_CHUNKS) for a in range(HALVES)])
            pe.wait_ge(wt_hi, 1)
            pe.wait_ge(wt_lo, 1)
            transpose_chunk([(h_banks[:, 0, a * LAT:(a + 1) * LAT], raw_fc1[:, a * P:(a + 1) * P], P)
                             for a in range(HALVES)]
                            + [(h_banks[:, 0, H + a * P:H + (a + 1) * P], raw_fc2[:, a, :], P)
                               for a in range(HALVES)]
                            + [(h_banks[:, 0, 2 * H + a * EXPERTS:2 * H + (a + 1) * EXPERTS],
                                raw_gate[:, a * P:(a + 1) * P], EXPERTS) for a in range(HALVES)])
            with pe.Fori(0, W_CHUNKS // 4) as i:
                for j in range(4):
                    slot = (SMALL_CHUNKS + j) % 2
                    pe.wait_ge(raw_loaded[j], (i + 1) * 2 * DMA)
                    pe.wait_ge(wt_hi, 4 * i + (SMALL_SPLITS + j - 1))
                    pe.wait_ge(wt_lo, 4 * i + (SMALL_SPLITS + j - 1))
                    transpose_chunk([(h_banks[:, slot, (w * W_CHUNK + e) * P:(w * W_CHUNK + e + 1) * P],
                                      raw_experts[:, j, w, e], P)
                                     for w in range(2) for e in range(W_CHUNK)])
            pe.wait_ge(wt_hi, SPLITS)
            pe.wait_ge(wt_lo, SPLITS)

            def project(p, b):
                pe.wait_ge(x_loaded[b], (p + 1) * DMA)
                pe.wait_ge(cond_loaded, (p + 1) * (BATCH_TILE * DMA))
                if b >= 2:
                    pe.wait_ge(xc_hi_ready, p * BLOCKS + b - 1)
                    pe.wait_ge(xc_lo_ready, p * BLOCKS + b - 1)
                for a in range(HALVES):
                    for g in range(BT):
                        last = pe.matmul(y_banks[:, b % 2, a * BANK + g * P:a * BANK + (g + 1) * P],
                                         x_in[:, b * BT + g, a * P:(a + 1) * P], cond_bd[:, b * BT + g, :],
                                         start=True, stop=True)
                last.then_inc(xc_ready, 1)

            def gate_and_latent(p, b):
                pe.wait_ge(xc_hi_ready, p * BLOCKS + b + 1)
                pe.wait_ge(xc_lo_ready, p * BLOCKS + b + 1)
                if b < 2:
                    pe.wait_ge(routed_added, p * BLOCKS)
                else:
                    pe.wait_ge(lat_hi_ready, p * BLOCKS + b - 1)
                    pe.wait_ge(lat_lo_ready, p * BLOCKS + b - 1)
                    pe.wait_ge(scores_t_ready, p * BLOCKS + b - 1)
                terms = [(w[:, GATE0 + a * P:GATE0 + (a + 1) * P], v[:, a, b * BANK:(b + 1) * BANK])
                         for a in range(HALVES) for w in (small_hi, small_lo) for v in (xc_hi, xc_lo)]
                for n, (w, v) in enumerate(terms):
                    last = pe.matmul(h_banks[:, b % 2, BANK:2 * BANK], w, v, start=n == 0, stop=n == len(terms) - 1)
                last.then_inc(logits_ready, 1)
                terms = [t for a in range(HALVES) for t in three(
                    *(w[:, FC1_0 + a * LAT:FC1_0 + (a + 1) * LAT] for w in (small_hi, small_lo)),
                    *(v[:, a, b * BANK:(b + 1) * BANK] for v in (xc_hi, xc_lo)))]
                for n, (w, v) in enumerate(terms):
                    last = pe.matmul(h_banks[:, b % 2, 0:BANK], w, v, start=n == 0, stop=n == len(terms) - 1)
                last.then_inc(lat_ready, 1)

            def shared_up(p, u):
                b = u // 2
                if u < 2:
                    pe.wait_ge(lat_hi_ready, p * BLOCKS + u + 3)
                    pe.wait_ge(lat_lo_ready, p * BLOCKS + u + 3)
                    pe.wait_ge(scores_t_ready, p * BLOCKS + u + 3)
                else:
                    pe.wait_ge(relu_ready, p * SHARED_UNITS + u - 1)
                for m in range(2):
                    k = 2 * (u % 2) + m
                    terms = [t for a in range(HALVES) for t in three(
                        *(w[:, UP0 + a * SHARED + k * P:UP0 + a * SHARED + (k + 1) * P] for w in (small_hi, small_lo)),
                        *(v[:, a, b * BANK:(b + 1) * BANK] for v in (xc_hi, xc_lo)))]
                    for n, (w, v) in enumerate(terms):
                        last = pe.matmul(h_banks[:, u % 2, m * BANK:(m + 1) * BANK], w, v,
                                         start=n == 0, stop=n == len(terms) - 1)
                last.then_inc(h_ready, 1)

            def shared_down(p, b):
                pe.wait_ge(act_hi_ready, p * UNITS + 2 * b + 2)
                pe.wait_ge(act_lo_ready, p * UNITS + 2 * b + 2)
                pe.wait_ge(shared_added, p * BLOCKS + b)
                for j in range(BT):
                    terms = []
                    for k in range(SHARED_CHUNKS):
                        cols = slice((k % 2) * BANK + j * P, (k % 2) * BANK + (j + 1) * P)
                        terms += three(act_hi[:, k // 2, cols], act_lo[:, k // 2, cols],
                                       *(w[:, DOWN0 + k * H:DOWN0 + (k + 1) * H] for w in (small_hi, small_lo)))
                    for n, (v, w) in enumerate(terms):
                        last = pe.matmul(y_banks[:, 0, j * H:(j + 1) * H], v, w,
                                         start=n == 0, stop=n == len(terms) - 1)
                last.then_inc(down_done, 1)

            def transpose_scores(p):
                pe.wait_ge(scores_t_ready, (p + 1) * BLOCKS)
                for n in range(TILES):
                    last = pe.matmul(y_banks[:, 1, n * EXPERTS:(n + 1) * EXPERTS], scores_t[:, n * P:(n + 1) * P],
                                     ident[0:EXPERTS, 0:EXPERTS], start=True, stop=True)
                last.then_inc(scores_transposed, 1)

            def transpose_s(p):
                pe.wait_ge(s_ready, p + 1)
                for b in range(BLOCKS):
                    last = pe.transpose(y_banks[:, 1, BANK + b * P:BANK + (b + 1) * P],
                                        s_tok[:, BT * b:BT * (b + 1), :].rearrange("t j e -> t (j e)"), ident[:, :])
                last.then_inc(s_t_ready, 1)

            def expert_up(p, slot, half, loads, unit):
                if half == 0:
                    pe.wait_ge(w1_loaded[slot], loads * DMA)
                if isinstance(unit, int):
                    pe.wait_ge(relu_ready, (p + 1) * SHARED_UNITS - 1 + unit)
                else:
                    pe.wait_ge(scaled_ready, unit - 1)
                for m in range(2):
                    cols = slice(half * UNIT + m * BANK, half * UNIT + (m + 1) * BANK)
                    terms = three(w1_ring[:, slot, 0], w1_ring[:, slot, 1], lat_hi[:, cols], lat_lo[:, cols])
                    for n, (w, v) in enumerate(terms):
                        last = pe.matmul(h_banks[:, half, m * BANK:(m + 1) * BANK], w, v, start=n == 0, stop=n == 2)
                last.then_inc(h_ready, 1)

            def expert_down(p, slot, half, loads, unit, first_expert, last_expert):
                if half == 0:
                    pe.wait_ge(w2_loaded[slot], loads * DMA)
                pe.wait_ge(act_hi_ready, unit + 1)
                terms = three(w2_ring[:, slot, 0], w2_ring[:, slot, 1], act_hi[:, half, :], act_lo[:, half, :])
                for n, (w, v) in enumerate(terms):
                    if n == 2:
                        pe.wait_ge(act_lo_ready, unit + 1)
                    for m in range(2):
                        last = pe.matmul(y_banks[:, half, m * BANK:(m + 1) * BANK], w, v[:, m * BANK:(m + 1) * BANK],
                                         start=first_expert and n == 0, stop=last_expert and n == 2)
                last.then_inc(experts_done, 1)

            def expert_pair(p, i, first_pair=False, last_pair=False):
                loads = p * (EXPERTS // 2) + i
                unit = p * EXPERT_UNITS + 4 * i
                act_unit = p * UNITS + SHARED_UNITS + 4 * i
                for k in range(2):
                    for half in range(TOKEN_HALVES):
                        if not (last_pair and k == 1):
                            expert_up(p, 1 - k, half, loads + (1 + k), unit + (2 * k + 2 + half))
                        expert_down(p, k, half, loads + 1, act_unit + (2 * k + half),
                                    first_pair and k == 0, last_pair and k == 1)

            def fc2(p, q):
                half = q // 2
                pe.wait_ge(y_hi_ready, p * TOKEN_HALVES + half + 1)
                pe.wait_ge(y_lo_ready, p * TOKEN_HALVES + half + 1)
                if q < 2:
                    pe.wait_ge(scaled_ready, (p + 1) * EXPERT_UNITS - 1 + q)
                else:
                    pe.wait_ge(routed_added, p * BLOCKS + q - 1)
                for j in range(BT):
                    cols = slice((q % 2) * BANK + j * P, (q % 2) * BANK + (j + 1) * P)
                    terms = three(act_hi[:, half, cols], act_lo[:, half, cols],
                                  small_hi[:, FC2_0:FC2_0 + H], small_lo[:, FC2_0:FC2_0 + H])
                    for n, (v, w) in enumerate(terms):
                        last = pe.matmul(h_banks[:, q % 2, j * H:(j + 1) * H], v, w, start=n == 0, stop=n == 2)
                last.then_inc(fc2_done, 1)

            with pe.Fori(0, PASSES) as p:
                project(p, 0)
                project(p, 1)
                gate_and_latent(p, 0)
                project(p, 2)
                gate_and_latent(p, 1)
                project(p, 3)
                gate_and_latent(p, 2)
                gate_and_latent(p, 3)
                shared_up(p, 0)
                transpose_scores(p)
                for u in range(1, 4):
                    shared_up(p, u)
                shared_down(p, 0)
                shared_up(p, 4)
                shared_up(p, 5)
                shared_down(p, 1)
                transpose_s(p)
                shared_up(p, 6)
                shared_up(p, 7)
                shared_down(p, 2)
                for half in range(TOKEN_HALVES):
                    expert_up(p, 0, half, p * (EXPERTS // 2) + 1, half)
                shared_down(p, 3)
                pe.wait_ge(shared_added, (p + 1) * BLOCKS)
                pe.wait_ge(s_t_copied, p + 1)
                expert_pair(p, 0, first_pair=True)
                with pe.Fori(1, EXPERTS // 2 - 1) as i:
                    expert_pair(p, i)
                expert_pair(p, EXPERTS // 2 - 1, last_pair=True)
                for q in range(BLOCKS):
                    fc2(p, q)

        @block.scalar
        def _(act):
            def round_chunk(c, dst, n):
                act.wait_ge(wt_ready, c + 1)
                act.activation(dst, h_banks[:, c % 2, 0:n], ACT.Copy).then_inc(wt_hi, 1)

            round_chunk(0, small_hi[:, UP0:DOWN0], DOWN0 - UP0)
            round_chunk(1, small_hi[:, DOWN0:FC1_0], FC1_0 - DOWN0)
            round_chunk(2, small_hi[:, FC1_0:GATE0], GATE0 - FC1_0)
            act.wait_ge(gate_zeroed, 2)
            act.activation(small_hi[:, GATE0:SMALL].rearrange("q (a e) -> q a e", a=HALVES)[:, :, 0:EXPERTS],
                           h_banks[:, 0, 2 * H:2 * H + HALVES * EXPERTS].rearrange("q (a e) -> q a e", a=HALVES),
                           ACT.Copy).then_inc(wt_hi, 1)
            with act.Fori(0, W_CHUNKS // 2) as i:
                for s in range(2):
                    act.wait_ge(w_stored[s], i * (4 * DMA))
                    act.wait_ge(wt_ready, 2 * i + (SMALL_CHUNKS + s + 1))
                    act.activation(act_hi[:, s, :], h_banks[:, (SMALL_CHUNKS + s) % 2, :], ACT.Copy)\
                        .then_inc(wt_hi, 1)

            def round_projection(p, b):
                act.wait_ge(xc_ready, p * BLOCKS + b + 1)
                act.activation(xc_hi[:, :, b * BANK:(b + 1) * BANK],
                               y_banks[:, b % 2, :].rearrange("q (a t) -> q a t", a=HALVES), ACT.Copy)\
                    .then_inc(xc_hi_ready, 1)

            def score_and_round_latent(p, b):
                act.wait_ge(logits_ready, p * BLOCKS + b + 1)
                act.activation(scores_t[:, b * BANK:(b + 1) * BANK], h_banks[0:EXPERTS, b % 2, BANK:2 * BANK],
                               ACT.Sigmoid).then_inc(scores_t_ready, 1)
                act.wait_ge(lat_ready, p * BLOCKS + b + 1)
                act.activation(lat_hi[:, b * BANK:(b + 1) * BANK], h_banks[:, b % 2, 0:BANK], ACT.Copy)\
                    .then_inc(lat_hi_ready, 1)

            def square(slot, taken):
                act.activation(act_hi[:, slot, :], scaled[:, slot, :], ACT.Square).then_inc(act_hi_ready, 1)
                act.wait_ge(act_lo_ready, taken)
                act.activation(act_full[:, slot, :], scaled[:, slot, :], ACT.Square).then_inc(act_full_ready, 1)

            def square_shared(p, u):
                before_slot = p * UNITS + (u - 1 if u >= 2 else 0)
                act.wait_ge(h_ready, p * UNITS + u + 1)
                act.wait_ge(act_full_ready, before_slot)
                act.activation(scaled[:, u % 2, :], h_banks[:, u % 2, :], ACT.Relu).then_inc(relu_ready, 1)
                act.wait_ge(relu_ready, p * SHARED_UNITS + u + 1)
                if u < 2:
                    act.wait_ge(fc2_done, p * BLOCKS)
                else:
                    act.wait_ge(down_done, p * BLOCKS + u // 2)
                square(u % 2, before_slot)

            for s in range(2):
                act.wait_ge(w_stored[s], 4 * DMA * (W_CHUNKS // 2))
            with act.Fori(0, PASSES) as p:
                round_projection(p, 0)
                round_projection(p, 1)
                score_and_round_latent(p, 0)
                round_projection(p, 2)
                score_and_round_latent(p, 1)
                round_projection(p, 3)
                score_and_round_latent(p, 2)
                score_and_round_latent(p, 3)
                square_shared(p, 0)
                act.wait_ge(scores_transposed, p + 1)
                act.activation(scores[:, :, :].rearrange("q n e -> q (n e)"), y_banks[:, 1, 0:BANK], ACT.Copy)\
                    .then_inc(scores_ready, 1)
                square_shared(p, 1)
                act.wait_ge(cw_ready, p + 1)
                act.activation(root[:, :, :], masked[:, :, :], ACT.Sqrt, scale=0.25).then_inc(root_ready, 1)
                for u in range(2, 6):
                    square_shared(p, u)
                act.wait_ge(s_t_ready, p + 1)
                act.wait_ge(s_stored, p * (BT * DMA))
                act.activation(s_t[:, :], y_banks[:, 1, BANK:2 * BANK], ACT.Copy).then_inc(s_t_copied, 1)
                square_shared(p, 6)
                square_shared(p, 7)
                base = p * UNITS + SHARED_UNITS
                for half in range(TOKEN_HALVES):
                    act.wait_ge(down_done, (p + 1) * BLOCKS)
                    act.wait_ge(scaled_ready, p * EXPERT_UNITS + half + 1)
                    square(half, base + half - 1)
                with act.Fori(1, EXPERTS) as e:
                    for half in range(TOKEN_HALVES):
                        act.wait_ge(scaled_ready, p * EXPERT_UNITS + 2 * e + (half + 1))
                        act.wait_ge(experts_done, p * EXPERT_UNITS + 2 * e + (half - 1))
                        square(half, base + 2 * e + (half - 1))
                for half in range(TOKEN_HALVES):
                    act.wait_ge(experts_done, (p + 1) * EXPERT_UNITS - 1 + half)
                    act.activation(act_hi[:, half, :], y_banks[:, half, :], ACT.Copy).then_inc(y_hi_ready, 1)

        @block.vector
        def _(dve):
            def rest_of_chunk(c, dst, hi, n):
                dve.wait_ge(wt_hi, c + 1)
                dve.tensor_tensor(dst, h_banks[:, c % 2, 0:n], hi.bitcast(f32), ALU.subtract).then_inc(wt_lo, 1)

            for c, (a, z) in enumerate(((UP0, DOWN0), (DOWN0, FC1_0), (FC1_0, GATE0))):
                rest_of_chunk(c, small_lo[:, a:z], small_hi[:, a:z], z - a)
            dve.wait_ge(gate_zeroed, 2)
            dve.wait_ge(wt_hi, SMALL_SPLITS)
            dve.tensor_tensor(small_lo[:, GATE0:SMALL].rearrange("q (a e) -> q a e", a=HALVES)[:, :, 0:EXPERTS],
                              h_banks[:, 0, 2 * H:2 * H + HALVES * EXPERTS].rearrange("q (a e) -> q a e", a=HALVES),
                              small_hi[:, GATE0:SMALL].rearrange("q (a e) -> q a e", a=HALVES)[:, :, 0:EXPERTS]
                              .bitcast(f32), ALU.subtract).then_inc(wt_lo, 1)
            with dve.Fori(0, W_CHUNKS // 2) as i:
                for s in range(2):
                    dve.wait_ge(w_stored[s], i * (4 * DMA))
                    dve.wait_ge(wt_hi, 2 * i + (SMALL_SPLITS + s + 1))
                    dve.tensor_tensor(act_lo[:, s, :], h_banks[:, (SMALL_CHUNKS + s) % 2, :],
                                      act_hi[:, s, :].bitcast(f32), ALU.subtract).then_inc(wt_lo, 1)
            for s in range(2):
                dve.wait_ge(w_stored[s], 4 * DMA * (W_CHUNKS // 2))
            dve.wait_ge(bias_loaded, DMA)
            dve.wait_ge(consts_ready, 2)

            def rest_of_projection(p, b):
                dve.wait_ge(xc_hi_ready, p * BLOCKS + b + 1)
                cols = slice(b * BANK, (b + 1) * BANK)
                dve.tensor_tensor(xc_lo[:, :, cols], y_banks[:, b % 2, :].rearrange("q (a t) -> q a t", a=HALVES),
                                  xc_hi[:, :, cols].bitcast(f32), ALU.subtract).then_inc(xc_lo_ready, 1)

            def rest_of_latent(p, b):
                dve.wait_ge(lat_hi_ready, p * BLOCKS + b + 1)
                cols = slice(b * BANK, (b + 1) * BANK)
                dve.tensor_tensor(lat_lo[:, cols], h_banks[:, b % 2, 0:BANK], lat_hi[:, cols].bitcast(f32),
                                  ALU.subtract).then_inc(lat_lo_ready, 1)

            def relu_and_scale(half, scale_slot, loads, unit):
                dve.wait_ge(h_ready, unit + 1)
                dve.wait_ge(scale_loaded[scale_slot], loads * DMA)
                dve.wait_ge(act_full_ready, unit - 1)
                dve.scalar_tensor_tensor(scaled[:, half, :], h_banks[:, half, :], 0.0, scale_ring[:, scale_slot, :],
                                         ALU.max, ALU.mult).then_inc(scaled_ready, 1)

            def rest(slot, unit):
                dve.wait_ge(act_hi_ready, unit + 1)
                dve.wait_ge(act_full_ready, unit + 1)
                dve.tensor_tensor(act_lo[:, slot, :], act_full[:, slot, :], act_hi[:, slot, :].bitcast(f32),
                                  ALU.subtract).then_inc(act_lo_ready, 1)

            def add_shared(p, b):
                dve.wait_ge(down_done, p * BLOCKS + b + 1)
                dve.wait_ge(out_stored[b], p * DMA)
                tiles = slice(BT * b, BT * (b + 1))
                dve.tensor_tensor(x_res[:, tiles, :], y_banks[:, 0, :].rearrange("q (j h) -> q j h", h=H),
                                  x_in[:, tiles, :], ALU.add).then_inc(shared_added, 1)

            steps = [0]

            def step(instruction):
                instruction.then_inc(gate_step, 1)
                steps[0] += 1

            def steps_done(p):
                dve.wait_ge(gate_step, p * GATE_STEPS + steps[0])

            def grouped(t):
                return t[:, :, :].rearrange("q n (g k) -> q (n g) k", g=GROUPS)

            def per_group(t):
                return t[:, :, :].rearrange("q n g -> q (n g)")

            def over_group(t):
                return per_group(t).unsqueeze(2).to_broadcast([P, TILES * GROUPS, GROUP_SIZE])

            def group_scores(p):
                dve.wait_ge(scores_ready, p + 1)
                step(dve.tensor_tensor(biased[:, :, :], scores[:, :, :],
                                       bias_sb[:, :].unsqueeze(1).to_broadcast([P, TILES, EXPERTS]), ALU.add))
                steps_done(p)
                step(dve.tensor_reduce(per_group(first), grouped(biased), AX.X, ALU.max))
                steps_done(p)
                step(dve.tensor_tensor(grouped(work), grouped(biased), over_group(first), ALU.is_equal))
                steps_done(p)
                step(dve.tensor_reduce(per_group(count), grouped(work), AX.X, ALU.add))
                step(dve.scalar_tensor_tensor(grouped(left), grouped(work), -BIG, grouped(biased), ALU.mult, ALU.add))
                steps_done(p)
                step(dve.tensor_reduce(per_group(second), grouped(left), AX.X, ALU.max))
                step(dve.tensor_scalar(per_group(count), per_group(count), 1.5, -BIG, ALU.is_lt, ALU.mult))
                steps_done(p)
                step(dve.tensor_tensor(per_group(count), per_group(count), per_group(first), ALU.add))
                steps_done(p)
                step(dve.tensor_tensor(per_group(second), per_group(second), per_group(count), ALU.max))
                steps_done(p)
                step(dve.tensor_tensor(per_group(group_score), per_group(first), per_group(second), ALU.add))
                steps_done(p)

            def pick_groups(p):
                full = [P, TILES, GROUPS, GROUPS]
                other = group_score[:, :, :].unsqueeze(2).to_broadcast(full)
                own = group_score[:, :, :].unsqueeze(3).to_broadcast(full)
                step(dve.tensor_tensor(group_gt[:, :, :, :], other, own, ALU.is_gt))
                step(dve.tensor_tensor(group_eq[:, :, :, :], other, own, ALU.is_equal))
                steps_done(p)
                step(dve.tensor_tensor(group_eq[:, :, :, :], group_eq[:, :, :, :],
                                       before[:, :, :].unsqueeze(1).to_broadcast(full), ALU.mult))
                steps_done(p)
                step(dve.tensor_tensor(group_gt[:, :, :, :], group_gt[:, :, :, :], group_eq[:, :, :, :], ALU.add))
                steps_done(p)
                step(dve.tensor_reduce(per_group(count), group_gt[:, :, :, :].rearrange("q n g k -> q (n g) k"),
                                       AX.X, ALU.add))
                steps_done(p)
                step(dve.tensor_scalar(per_group(count), per_group(count), TOP_GROUPS - 0.5, -BIG,
                                       ALU.is_gt, ALU.mult))
                steps_done(p)
                step(dve.tensor_tensor(grouped(masked), grouped(biased), over_group(count), ALU.add))
                steps_done(p)

            def largest(tiles):
                for n in tiles:
                    step(dve.max(top8[:, n, :], masked[:, n, :]))

            def mark(tiles):
                for n in tiles:
                    step(dve.match_replace(left[:, n, :], top8[:, n, :], masked[:, n, :], TAKEN))

            def combine_weights(p):
                step(dve.scalar_tensor_tensor(work[:, :, :], left[:, :, :], TAKEN, scores[:, :, :],
                                              ALU.is_equal, ALU.mult))
                steps_done(p)
                step(dve.tensor_reduce(total[:, :], work[:, :, :], AX.X, ALU.add))
                steps_done(p)
                step(dve.reciprocal(total[:, :], total[:, :]))
                steps_done(p)
                step(dve.scalar_tensor_tensor(cw[:, :, :], work[:, :, :], ROUTED_SCALE,
                                              total[:, :].unsqueeze(2).to_broadcast([P, TILES, EXPERTS]),
                                              ALU.mult, ALU.mult))
                steps_done(p)
                dve.tensor_scalar(masked[:, :, :], cw[:, :, :], TINY, None, ALU.max).then_inc(cw_ready, 1)

            def root_of_weights(p):
                dve.wait_ge(root_ready, p + 1)
                step(dve.reciprocal(left[:, :, :], root[:, :, :]))
                steps_done(p)
                step(dve.tensor_tensor(left[:, :, :], left[:, :, :], cw[:, :, :], ALU.mult))
                steps_done(p)
                step(dve.scalar_tensor_tensor(left[:, :, :], left[:, :, :], 0.25, root[:, :, :], ALU.mult, ALU.add))
                steps_done(p)
                dve.scalar_tensor_tensor(s_tok[:, :, :], cw[:, :, :], 0.0, left[:, :, :],
                                         ALU.is_gt, ALU.mult).then_inc(s_ready, 1)

            with dve.Fori(0, PASSES) as p:
                rest_of_projection(p, 0)
                rest_of_projection(p, 1)
                rest_of_latent(p, 0)
                rest_of_projection(p, 2)
                rest_of_latent(p, 1)
                rest_of_projection(p, 3)
                rest_of_latent(p, 2)
                rest_of_latent(p, 3)
                shared = p * UNITS
                group_scores(p)
                pick_groups(p)
                rest(0, shared)
                largest(range(TILES))
                steps_done(p)
                rest(1, shared + 1)
                mark(range(TILES))
                steps_done(p)
                combine_weights(p)
                add_shared(p, 0)
                root_of_weights(p)
                rest(0, shared + 2)
                rest(1, shared + 3)
                add_shared(p, 1)
                rest(0, shared + 4)
                rest(1, shared + 5)
                add_shared(p, 2)
                rest(0, shared + 6)
                base = p * UNITS + SHARED_UNITS
                loads = p * (EXPERTS // 2)
                relu_and_scale(0, 0, loads + 1, base)
                rest(1, shared + 7)
                relu_and_scale(1, 1, loads + 1, base + 1)
                add_shared(p, 3)
                with dve.Fori(0, EXPERTS // 2 - 1) as i:
                    for u in range(4):
                        unit = base + 4 * i + u
                        rest(u % 2, unit)
                        relu_and_scale(u % 2, (u + 2) % 4, loads + i + (1 if u < 2 else 2), unit + 2)
                for u in range(EXPERT_UNITS - 4, EXPERT_UNITS):
                    rest(u % 2, base + u)
                    if u + 2 < EXPERT_UNITS:
                        relu_and_scale(u % 2, (u + 2) % 4, loads + EXPERTS // 2, base + u + 2)
                for half in range(TOKEN_HALVES):
                    dve.wait_ge(y_hi_ready, p * TOKEN_HALVES + half + 1)
                    dve.tensor_tensor(act_lo[:, half, :], y_banks[:, half, :], act_hi[:, half, :].bitcast(f32),
                                      ALU.subtract).then_inc(y_lo_ready, 1)
                for q in range(BLOCKS):
                    dve.wait_ge(fc2_done, p * BLOCKS + q + 1)
                    tiles = slice(BT * q, BT * (q + 1))
                    dve.tensor_tensor(x_res[:, tiles, :], h_banks[:, q % 2, :].rearrange("q (j h) -> q j h", h=H),
                                      x_res[:, tiles, :], ALU.add).then_inc(routed_added, 1)
            assert steps[0] == GATE_STEPS


def kernel(x, itok_B_1_198, L0_cond_weights, L0_ffn_gate_w, L0_ffn_gate_bias, L0_ffn_fc1_w, L0_ffn_fc2_w,
           L0_ffn_w1, L0_ffn_w2, L0_ffn_shared_up_w, L0_ffn_shared_down_w):
    import numpy as np
    import concourse.bacc as bacc
    from concourse.bass_utils import run_bass_kernel_spmd

    given = {"x": x, "cond": itok_B_1_198, "cond_w": L0_cond_weights, "gate_w": L0_ffn_gate_w,
             "gate_b": L0_ffn_gate_bias, "fc1_w": L0_ffn_fc1_w, "fc2_w": L0_ffn_fc2_w, "w1": L0_ffn_w1,
             "w2": L0_ffn_w2, "up_w": L0_ffn_shared_up_w, "down_w": L0_ffn_shared_down_w}
    nc = bacc.Bacc("TRN2", target_bir_lowering=False, num_devices=1)
    arrays, args = {}, {}
    for name, value in given.items():
        a = np.ascontiguousarray(value)
        arrays[f"in_{name}"] = a
        args[name] = nc.dram_tensor(f"in_{name}", a.shape, mybir.dt.from_np(a.dtype), kind="ExternalInput").ap()
    out = nc.dram_tensor("out_x", (B, C, H), mybir.dt.float32, kind="ExternalOutput").ap()
    adaln_ffn(nc, **args, out=out)
    result = run_bass_kernel_spmd(nc, [arrays], core_ids=[0])
    return result.results[0]["out_x"]
```

```python
from contextlib import ExitStack

import concourse.bass as bass
from concourse import mybir

B, C, H = 128, 32, 256
STATES = 200
EXPERTS, LAT, INTER = 32, 128, 128
GROUPS, TOP_GROUPS, TOP_K = 4, 2, 8
GROUP_SIZE = EXPERTS // GROUPS
SHARED = 512
ROUTED_SCALE = 2.5
P = 128
TOKENS = B * C
PASSES = 2
PASS_TOKENS = TOKENS // PASSES
BANK = 512
BLOCKS = PASS_TOKENS // BANK
TILES = PASS_TOKENS // P
BT = TILES // BLOCKS
BATCH_TILE = P // C
HALVES = H // P
TILES_OF_BANK = BANK // H
UNIT = 2 * BANK
SHARED_CHUNKS = SHARED // P
SHARED_UNITS = BLOCKS * 2
TOKEN_HALVES = PASS_TOKENS // UNIT
EXPERT_UNITS = EXPERTS * TOKEN_HALVES
UNITS = SHARED_UNITS + EXPERT_UNITS
W_CHUNK = 4
W_CHUNKS = EXPERTS // W_CHUNK
SMALL_SPLITS = 4
RAW_EXPERTS = 8
RAW_LOADS = EXPERTS // RAW_EXPERTS
ROOT_BEHIND = 3
TRANSPOSE_S_BEHIND = 6
BIG = 1e38
TAKEN = -3e38
TINY = 1e-30
DMA = 16

UP0 = 0
DOWN0 = UP0 + HALVES * SHARED
FC1_0 = DOWN0 + SHARED_CHUNKS * H
FC2_0 = FC1_0 + HALVES * LAT
GATE0 = FC2_0 + H
SMALL = GATE0 + HALVES * P


def adaln_ffn(nc, x, cond, cond_w, gate_w, gate_b, fc1_w, fc2_w, w1, w2, up_w, down_w, out):
    f32, f32r, i32 = mybir.dt.float32, mybir.dt.float32r, mybir.dt.int32
    ALU, ACT, AX = mybir.AluOpType, mybir.ActivationFunctionType, mybir.AxisListType

    x_rows = x.rearrange("b c h -> (b c) h").rearrange("(n p) h -> p n h", p=P)
    out_rows = out.rearrange("b c h -> (b c) h").rearrange("(n p) h -> p n h", p=P)

    cond_dram = nc.dram_tensor("cond_dram", (B, C, C), f32).ap()
    s_dram = nc.dram_tensor("s_dram", (EXPERTS, PASS_TOKENS), f32).ap()

    with ExitStack() as ctx:
        def sb(name, shape, dt=f32):
            return ctx.enter_context(nc.sbuf_tensor(name, shape, dt))

        def sem(name):
            return ctx.enter_context(nc.semaphore(name))

        def sems(name, n):
            return [sem(f"{name}{i}") for i in range(n)]

        x_in = sb("x_in", [P, TILES, H])
        x_res = sb("x_res", [P, TILES, H])
        cond_bd = sb("cond_bd", [P, TILES, P])
        cond_sb = sb("cond_sb", [B, 1], i32)
        xc_hi = sb("xc_hi", [P, HALVES, PASS_TOKENS], f32r)
        xc_lo = sb("xc_lo", [P, HALVES, PASS_TOKENS], f32r)
        lat_hi = sb("lat_hi", [P, PASS_TOKENS], f32r)
        lat_lo = sb("lat_lo", [P, PASS_TOKENS], f32r)
        small_hi = sb("small_hi", [P, SMALL], f32r)
        small_lo = sb("small_lo", [P, SMALL], f32r)
        experts_w = sb("experts_w", [P, 2, EXPERTS, P])
        w1_ring = sb("w1_ring", [P, 2, 2, P], f32r)
        w2_ring = sb("w2_ring", [P, 2, 2, P], f32r)
        unsplit = sb("unsplit", [P, 2, 2, P])
        scale_ring = sb("scale_ring", [P, 4, UNIT])
        scaled = sb("scaled", [P, 2, UNIT])
        act_full = sb("act_full", [P, 2, UNIT])
        act_hi = sb("act_hi", [P, 2, UNIT], f32r)
        act_lo = sb("act_lo", [P, 2, UNIT], f32r)
        s_t = sb("s_t", [P, BANK])
        ident = sb("ident", [P, P])
        bias_sb = sb("bias_sb", [P, EXPERTS])
        zero = sb("zero", [P, 1])
        table_load = sb("table_load", [P, 1])
        before = sb("before", [P, GROUPS, GROUPS])
        scores, biased, work, masked, left, cw, root, s_tok = (
            scale_ring[:, n // 2, (n % 2) * BANK:(n % 2 + 1) * BANK].rearrange("q (n e) -> q n e", e=EXPERTS)
            for n in range(8))
        top8 = sb("top8", [P, TILES, 8])
        first = sb("first", [P, TILES, GROUPS])
        count = sb("count", [P, TILES, GROUPS])
        second = sb("second", [P, TILES, GROUPS])
        group_score = sb("group_score", [P, TILES, GROUPS])
        group_gt = sb("group_gt", [P, TILES, GROUPS, GROUPS])
        group_eq = sb("group_eq", [P, TILES, GROUPS, GROUPS])
        total = sb("total", [P, TILES])

        raw_up = scaled[:, 0, :].rearrange("p (k h) -> p k h", h=H)
        raw_down = scaled[:, 1, :].rearrange("p (a m) -> p a m", m=SHARED)
        raw_fc1 = act_full[:, 0, 0:H]
        raw_fc2 = act_full[:, 0, H:2 * H].rearrange("p (a l) -> p a l", l=LAT)
        raw_gate = act_full[0:EXPERTS, 0, 2 * H:3 * H]
        scores_t = act_full[:, 1, 0:BANK]
        cond_rows = scale_ring[:, 3, :]

        h_banks = ctx.enter_context(nc.psum_tensor("h_banks", [P, 2, UNIT], f32))
        y_banks = ctx.enter_context(nc.psum_tensor("y_banks", [P, 2, UNIT], f32))

        def per_half(t):
            return t.rearrange("q (a e) -> q a e", a=HALVES)

        gate_banks = per_half(y_banks[:, 0, 2 * H:2 * H + HALVES * EXPERTS])

        def gate_columns(weights):
            return per_half(weights[:, GATE0:SMALL])[:, :, 0:EXPERTS]

        x_loaded = sems("x_loaded", BLOCKS)
        cond_idx_loaded = sem("cond_idx_loaded")
        bias_loaded = sem("bias_loaded")
        up_loaded = sem("up_loaded")
        down_loaded = sem("down_loaded")
        small_loaded = sem("small_loaded")
        raw_loaded = sems("raw_loaded", RAW_LOADS)
        cond_gathered = sem("cond_gathered")
        cond_stored = sem("cond_stored")
        cond_loaded = sem("cond_loaded")
        s_stored = sem("s_stored")
        scale_loaded = sems("scale_loaded", 4)
        out_stored = sems("out_stored", BLOCKS)
        const_step = sem("const_step")
        consts_ready = sem("consts_ready")
        cond_zeroed = sem("cond_zeroed")
        gate_zeroed = sem("gate_zeroed")
        split_step = sem("split_step")
        w1_split = sem("w1_split")
        w2_split = sem("w2_split")
        wt_ready = sem("wt_ready")
        experts_transposed = sem("experts_transposed")
        xc_ready = sem("xc_ready")
        logits_ready = sem("logits_ready")
        lat_ready = sem("lat_ready")
        h_ready = sem("h_ready")
        down_done = sem("down_done")
        scores_transposed = sem("scores_transposed")
        s_t_ready = sem("s_t_ready")
        experts_done = sem("experts_done")
        fc2_done = sem("fc2_done")
        table_loaded = sem("table_loaded")
        wt_hi = sem("wt_hi")
        experts_copied = sem("experts_copied")
        xc_hi_ready = sem("xc_hi_ready")
        lat_hi_ready = sem("lat_hi_ready")
        scores_t_ready = sem("scores_t_ready")
        scores_ready = sem("scores_ready")
        root_ready = sem("root_ready")
        relu_ready = sem("relu_ready")
        act_hi_ready = sem("act_hi_ready")
        act_full_ready = sem("act_full_ready")
        s_t_copied = sem("s_t_copied")
        y_hi_ready = sem("y_hi_ready")
        wt_lo = sem("wt_lo")
        xc_lo_ready = sem("xc_lo_ready")
        lat_lo_ready = sem("lat_lo_ready")
        gate_step = sem("gate_step")
        cw_ready = sem("cw_ready")
        s_ready = sem("s_ready")
        scaled_ready = sem("scaled_ready")
        act_lo_ready = sem("act_lo_ready")
        shared_added = sem("shared_added")
        y_lo_ready = sem("y_lo_ready")
        routed_added = sem("routed_added")

        block = ctx.enter_context(nc.Block())

        def three(w_hi, w_lo, v_hi, v_lo):
            return ((w_hi, v_hi), (w_lo, v_hi), (w_hi, v_lo))

        @block.sync
        def _(sp):
            sp.dma_start(cond_sb[:, :], cond.rearrange("(b a) -> b a", a=1)).then_inc(cond_idx_loaded, DMA)
            sp.dma_start(raw_up, up_w.rearrange("(k p) h -> p k h", p=P)).then_inc(up_loaded, DMA)
            sp.dma_start(raw_down, down_w.rearrange("(a p) m -> p a m", p=P)).then_inc(down_loaded, DMA)
            sp.dma_start(raw_fc1, fc1_w).then_inc(small_loaded, DMA)
            sp.dma_start(raw_fc2, fc2_w.rearrange("(a p) l -> p a l", p=P)).then_inc(small_loaded, DMA)
            sp.dma_start(raw_gate, gate_w).then_inc(small_loaded, DMA)

            def load_x(p, b):
                sp.dma_start(x_in[:, BT * b:BT * (b + 1), :],
                             x_rows[:, p * TILES + BT * b:p * TILES + BT * (b + 1), :]).then_inc(x_loaded[b], DMA)

            def load_cond(p):
                for j in range(BATCH_TILE):
                    sp.dma_start(
                        cond_bd[C * j:C * (j + 1), :, C * j:C * (j + 1)],
                        cond_dram[p * TILES * BATCH_TILE:(p + 1) * TILES * BATCH_TILE]
                        .rearrange("(g j) c d -> j c g d", j=BATCH_TILE)[j],
                    ).then_inc(cond_loaded, DMA)

            load_x(0, 0)
            sp.wait_ge(cond_gathered, DMA)
            sp.dma_start(cond_dram.rearrange("b c d -> b (c d)"), cond_rows).then_inc(cond_stored, DMA)
            load_x(0, 1)
            sp.wait_ge(cond_zeroed, 1)
            sp.wait_ge(cond_stored, DMA)
            load_cond(0)
            load_x(0, 2)
            load_x(0, 3)
            for c in range(RAW_LOADS):
                experts = slice(c * RAW_EXPERTS, (c + 1) * RAW_EXPERTS)
                for w, src in enumerate((w1, w2)):
                    sp.dma_start(experts_w[:, w, experts, :], src[experts].rearrange("e p i -> p e i"))\
                        .then_inc(raw_loaded[c], DMA)

            def load_scale(slot, e, half):
                src = s_dram[bass.ds(e, 1), half * UNIT:(half + 1) * UNIT]
                sp.dma_start(scale_ring[:, slot, :], src.to_broadcast([P, UNIT]))\
                    .then_inc(scale_loaded[slot], DMA)

            for p in range(PASSES):
                sp.wait_ge(s_t_copied, p + 1)
                for j in range(BT):
                    sp.dma_start(
                        s_dram.rearrange("e (b j t) -> j e b t", b=BLOCKS, j=BT)[j],
                        s_t[EXPERTS * j:EXPERTS * (j + 1), :].rearrange("e (b t) -> e b t", b=BLOCKS),
                    ).then_inc(s_stored, DMA)
                sp.wait_ge(s_stored, (p + 1) * BT * DMA)
                for slot in range(4):
                    load_scale(slot, slot // 2, slot % 2)
                if p + 1 < PASSES:
                    sp.wait_ge(xc_ready, (p + 1) * BLOCKS)
                    load_cond(p + 1)
                    for b in range(BLOCKS):
                        sp.wait_ge(shared_added, p * BLOCKS + b + 1)
                        load_x(p + 1, b)
                with sp.Fori(0, EXPERTS // 2 - 1) as i:
                    for slot in range(4):
                        sp.wait_ge(scaled_ready, 4 * i + (p * EXPERT_UNITS + slot + 1))
                        load_scale(slot, 2 * i + (slot // 2 + 2), slot % 2)
                for q in range(BLOCKS):
                    sp.wait_ge(routed_added, p * BLOCKS + q + 1)
                    sp.dma_start(out_rows[:, p * TILES + BT * q:p * TILES + BT * (q + 1), :],
                                 x_res[:, BT * q:BT * (q + 1), :]).then_inc(out_stored[q], DMA)
            for q in range(BLOCKS):
                sp.wait_ge(out_stored[q], PASSES * DMA)

        @block.gpsimd
        def _(pool):
            pool.memset(zero[:, :], 0.0).then_inc(const_step, 1)
            pool.memset(ident[:, :], 0.0).then_inc(const_step, 1)
            pool.memset(before[:, :, :], 0.0).then_inc(const_step, 1)
            pool.wait_ge(const_step, 3)
            pool.affine_select(out=ident[:, :], in_=ident[:, :], compare_op=ALU.not_equal, fill=1.0, base=0,
                               pattern=[[-1, P]], channel_multiplier=1).then_inc(consts_ready, 1)
            pool.wait_ge(cond_idx_loaded, DMA)
            pool.indirect_dma_start(
                cond_rows, None, cond_w.rearrange("s c d -> s (c d)"),
                bass.IndirectOffsetOnAxis(ap=cond_sb[:, 0:1], axis=0)).then_inc(cond_gathered, DMA)
            pool.dma_start(bias_sb[:, :], gate_b.rearrange("(a e) -> a e", a=1).to_broadcast([P, EXPERTS]))\
                .then_inc(bias_loaded, DMA)
            pool.affine_select(out=before[:, :, :], in_=before[:, :, :], compare_op=ALU.is_ge, fill=1.0, base=0,
                               pattern=[[-1, GROUPS], [1, GROUPS]], channel_multiplier=0).then_inc(consts_ready, 1)
            pool.memset(cond_bd[:, :, :], 0.0).then_inc(cond_zeroed, 1)
            pool.memset(small_hi[:, GATE0:SMALL].bitcast(f32), 0.0).then_inc(gate_zeroed, 1)
            pool.memset(small_lo[:, GATE0:SMALL].bitcast(f32), 0.0).then_inc(gate_zeroed, 1)

            def split(p, w, slot, e):
                ring, ready = ((w1_ring, w1_split), (w2_ring, w2_split))[w]
                source = experts_w[:, w, bass.ds(e, 1), :].rearrange("q a i -> q (a i)")
                pool.tensor_copy(unsplit[:, slot, w, :], source).then_inc(split_step, 1)
                pool.tensor_copy(ring[:, slot, 0, :], source).then_inc(split_step, 1)
                pool.wait_ge(split_step, 4 * e + (p * 4 * EXPERTS + 2 * w + 2))
                pool.tensor_tensor(ring[:, slot, 1, :], unsplit[:, slot, w, :], ring[:, slot, 0, :].bitcast(f32),
                                   ALU.subtract)\
                    .then_inc(ready, 1)

            for p in range(PASSES):
                if p == 0:
                    pool.wait_ge(experts_copied, 2 * W_CHUNKS)
                else:
                    pool.wait_ge(experts_done, p * EXPERT_UNITS)
                for slot in range(2):
                    for w in range(2):
                        split(p, w, slot, slot)
                with pool.Fori(0, EXPERTS // 2 - 1) as i:
                    for k in range(2):
                        pool.wait_ge(h_ready, 4 * i + (p * UNITS + SHARED_UNITS + 2 * k + 2))
                        split(p, 0, k, 2 * i + (k + 2))
                        pool.wait_ge(experts_done, 4 * i + (p * EXPERT_UNITS + 2 * k + 2))
                        split(p, 1, k, 2 * i + (k + 2))

        @block.tensor
        def _(pe):
            def transpose_chunk(jobs):
                for dst, src, n in jobs:
                    last = pe.transpose(dst, src, ident[0:n, 0:n])
                last.then_inc(wt_ready, 1)

            pe.wait_ge(consts_ready, 1)
            pe.wait_ge(up_loaded, DMA)
            transpose_chunk([(h_banks[:, 0, a * SHARED + k * P:a * SHARED + (k + 1) * P],
                              raw_up[:, k, a * P:(a + 1) * P], P)
                             for a in range(HALVES) for k in range(SHARED_CHUNKS)])
            pe.wait_ge(down_loaded, DMA)
            transpose_chunk([(h_banks[:, 1, k * H + a * P:k * H + (a + 1) * P],
                              raw_down[:, a, k * P:(k + 1) * P], P)
                             for k in range(SHARED_CHUNKS) for a in range(HALVES)])
            pe.wait_ge(small_loaded, 3 * DMA)
            transpose_chunk([(y_banks[:, 0, a * LAT:(a + 1) * LAT], raw_fc1[:, a * P:(a + 1) * P], P)
                             for a in range(HALVES)]
                            + [(y_banks[:, 0, H + a * P:H + (a + 1) * P], raw_fc2[:, a, :], P)
                               for a in range(HALVES)]
                            + [(y_banks[:, 0, 2 * H + a * EXPERTS:2 * H + (a + 1) * EXPERTS],
                                raw_gate[:, a * P:(a + 1) * P], EXPERTS) for a in range(HALVES)])

            def transpose_experts(n):
                c, w = divmod(n, 2)
                if n % (2 * RAW_EXPERTS // W_CHUNK) == 0:
                    pe.wait_ge(raw_loaded[c * W_CHUNK // RAW_EXPERTS], 2 * DMA)
                if n == 0:
                    pe.wait_ge(scores_ready, 1)
                if n >= 2:
                    pe.wait_ge(experts_copied, n - 1)
                for e in range(W_CHUNK):
                    last = pe.transpose(y_banks[:, 1, (n % 2) * BANK + e * P:(n % 2) * BANK + (e + 1) * P],
                                        experts_w[:, w, c * W_CHUNK + e, :], ident[:, :])
                last.then_inc(experts_transposed, 1)

            def project(p, b):
                pe.wait_ge(x_loaded[b], (p + 1) * DMA)
                pe.wait_ge(cond_loaded, (p + 1) * (BATCH_TILE * DMA))
                if b >= 2:
                    pe.wait_ge(xc_hi_ready, p * BLOCKS + b - 1)
                    pe.wait_ge(xc_lo_ready, p * BLOCKS + b - 1)
                elif p == 0:
                    pe.wait_ge(wt_hi, b + 1)
                    pe.wait_ge(wt_lo, b + 1)
                else:
                    pe.wait_ge(scaled_ready, p * EXPERT_UNITS - 1 + b)
                for a in range(HALVES):
                    for g in range(BT):
                        last = pe.matmul(h_banks[:, b % 2, a * BANK + g * P:a * BANK + (g + 1) * P],
                                         x_in[:, b * BT + g, a * P:(a + 1) * P], cond_bd[:, b * BT + g, :],
                                         start=True, stop=True)
                last.then_inc(xc_ready, 1)

            def gate_and_latent(p, b):
                pe.wait_ge(xc_hi_ready, p * BLOCKS + b + 1)
                pe.wait_ge(xc_lo_ready, p * BLOCKS + b + 1)
                if b >= 2:
                    pe.wait_ge(lat_hi_ready, p * BLOCKS + b - 1)
                    pe.wait_ge(lat_lo_ready, p * BLOCKS + b - 1)
                    pe.wait_ge(scores_t_ready, p * BLOCKS + b - 1)
                elif p == 0:
                    pe.wait_ge(wt_hi, SMALL_SPLITS)
                    pe.wait_ge(wt_lo, SMALL_SPLITS)
                else:
                    pe.wait_ge(routed_added, p * BLOCKS - 1 + b)
                terms = [(w[:, GATE0 + a * P:GATE0 + (a + 1) * P], v[:, a, b * BANK:(b + 1) * BANK])
                         for a in range(HALVES) for w in (small_hi, small_lo) for v in (xc_hi, xc_lo)]
                for n, (w, v) in enumerate(terms):
                    last = pe.matmul(y_banks[:, b % 2, BANK:2 * BANK], w, v, start=n == 0, stop=n == len(terms) - 1)
                last.then_inc(logits_ready, 1)
                terms = [t for a in range(HALVES) for t in three(
                    *(w[:, FC1_0 + a * LAT:FC1_0 + (a + 1) * LAT] for w in (small_hi, small_lo)),
                    *(v[:, a, b * BANK:(b + 1) * BANK] for v in (xc_hi, xc_lo)))]
                for n, (w, v) in enumerate(terms):
                    last = pe.matmul(y_banks[:, b % 2, 0:BANK], w, v, start=n == 0, stop=n == len(terms) - 1)
                last.then_inc(lat_ready, 1)

            def shared_up(p, u):
                b = u // 2
                if u < 2:
                    pe.wait_ge(xc_hi_ready, p * BLOCKS + u + 3)
                    pe.wait_ge(xc_lo_ready, p * BLOCKS + u + 3)
                else:
                    pe.wait_ge(relu_ready, p * SHARED_UNITS + u - 1)
                for m in range(2):
                    k = 2 * (u % 2) + m
                    terms = [t for a in range(HALVES) for t in three(
                        *(w[:, UP0 + a * SHARED + k * P:UP0 + a * SHARED + (k + 1) * P] for w in (small_hi, small_lo)),
                        *(v[:, a, b * BANK:(b + 1) * BANK] for v in (xc_hi, xc_lo)))]
                    for n, (w, v) in enumerate(terms):
                        last = pe.matmul(h_banks[:, u % 2, m * BANK:(m + 1) * BANK], w, v,
                                         start=n == 0, stop=n == len(terms) - 1)
                last.then_inc(h_ready, 1)

            def shared_down(p, u):
                b, slot = divmod(u, 2)
                pe.wait_ge(act_hi_ready, p * UNITS + u + 1)
                pe.wait_ge(act_lo_ready, p * UNITS + u + 1)
                if u == 0:
                    pe.wait_ge(lat_hi_ready, p * BLOCKS + 3)
                    pe.wait_ge(lat_lo_ready, p * BLOCKS + 3)
                elif slot == 0:
                    pe.wait_ge(shared_added, p * BLOCKS + b)
                for j in range(BT):
                    terms = []
                    for m in range(2):
                        k = 2 * slot + m
                        cols = slice(m * BANK + j * P, m * BANK + (j + 1) * P)
                        terms += three(act_hi[:, slot, cols], act_lo[:, slot, cols],
                                       *(w[:, DOWN0 + k * H:DOWN0 + (k + 1) * H] for w in (small_hi, small_lo)))
                    for n, (v, w) in enumerate(terms):
                        last = pe.matmul(y_banks[:, 0, j * H:(j + 1) * H], v, w,
                                         start=slot == 0 and j % TILES_OF_BANK == 0 and n == 0,
                                         stop=slot == 1 and j % TILES_OF_BANK == TILES_OF_BANK - 1
                                         and n == len(terms) - 1)
                last.then_inc(down_done, 1)

            def transpose_scores(p):
                pe.wait_ge(lat_hi_ready, (p + 1) * BLOCKS)
                pe.wait_ge(lat_lo_ready, (p + 1) * BLOCKS)
                pe.wait_ge(scores_t_ready, (p + 1) * BLOCKS)
                for j in range(BT):
                    last = pe.transpose(y_banks[:, 1, j * P:(j + 1) * P], scores_t[:, j * P:(j + 1) * P], ident[:, :])
                last.then_inc(scores_transposed, 1)

            def transpose_s(p):
                pe.wait_ge(experts_copied, 2 * W_CHUNKS)
                pe.wait_ge(s_ready, p + 1)
                for b in range(BLOCKS):
                    last = pe.transpose(y_banks[:, 1, BANK + b * P:BANK + (b + 1) * P],
                                        s_tok[:, BT * b:BT * (b + 1), :].rearrange("t j e -> t (j e)"), ident[:, :])
                last.then_inc(s_t_ready, 1)

            def transpose_pair(p, k):
                if p == 0 and k < W_CHUNKS:
                    transpose_experts(2 * k)
                    transpose_experts(2 * k + 1)

            def expert_up(slot, half, split_experts):
                if half == 0:
                    pe.wait_ge(w1_split, split_experts)
                for m in range(2):
                    cols = slice(half * UNIT + m * BANK, half * UNIT + (m + 1) * BANK)
                    terms = three(w1_ring[:, slot, 0], w1_ring[:, slot, 1], lat_hi[:, cols], lat_lo[:, cols])
                    for n, (w, v) in enumerate(terms):
                        last = pe.matmul(h_banks[:, half, m * BANK:(m + 1) * BANK], w, v, start=n == 0, stop=n == 2)
                last.then_inc(h_ready, 1)

            def expert_down(slot, half, split_experts, unit, first_expert=False, last_expert=False):
                if half == 0:
                    pe.wait_ge(w2_split, split_experts)
                pe.wait_ge(act_hi_ready, unit + 1)
                terms = three(w2_ring[:, slot, 0], w2_ring[:, slot, 1], act_hi[:, half, :], act_lo[:, half, :])
                for n, (w, v) in enumerate(terms):
                    if n == 2:
                        pe.wait_ge(act_lo_ready, unit + 1)
                    for m in range(2):
                        last = pe.matmul(y_banks[:, half, m * BANK:(m + 1) * BANK], w, v[:, m * BANK:(m + 1) * BANK],
                                         start=first_expert and n == 0, stop=last_expert and n == 2)
                last.then_inc(experts_done, 1)

            def up_and_down(p, e, k, first=False):
                unit = 2 * e + (p * UNITS + SHARED_UNITS + 2 * k)
                for half in range(TOKEN_HALVES):
                    pe.wait_ge(scaled_ready, 2 * e + (p * EXPERT_UNITS + 2 * k + half + 1))
                    expert_up((k + 1) % 2, half, e + (p * EXPERTS + k + 2))
                    expert_down(k % 2, half, e + (p * EXPERTS + k + 1), unit + half, first_expert=first)

            def fc2(p, q):
                half = q // 2
                pe.wait_ge(y_hi_ready, p * TOKEN_HALVES + half + 1)
                pe.wait_ge(y_lo_ready, p * TOKEN_HALVES + half + 1)
                if q == 1:
                    pe.wait_ge(y_lo_ready, p * TOKEN_HALVES + 2)
                elif q >= 2:
                    pe.wait_ge(routed_added, p * BLOCKS + q - 1)
                for j in range(BT):
                    cols = slice((q % 2) * BANK + j * P, (q % 2) * BANK + (j + 1) * P)
                    terms = three(act_hi[:, half, cols], act_lo[:, half, cols],
                                  small_hi[:, FC2_0:FC2_0 + H], small_lo[:, FC2_0:FC2_0 + H])
                    for n, (v, w) in enumerate(terms):
                        last = pe.matmul(y_banks[:, q % 2, j * H:(j + 1) * H], v, w, start=n == 0, stop=n == 2)
                last.then_inc(fc2_done, 1)

            project(0, 0)
            project(0, 1)
            for p in range(PASSES):
                if p == 0:
                    project(p, 2)
                    gate_and_latent(p, 0)
                    project(p, 3)
                    gate_and_latent(p, 1)
                else:
                    fc2(p - 1, 0)
                    fc2(p - 1, 1)
                    project(p, 2)
                    fc2(p - 1, 2)
                    project(p, 3)
                    fc2(p - 1, 3)
                    gate_and_latent(p, 0)
                    gate_and_latent(p, 1)
                gate_and_latent(p, 2)
                gate_and_latent(p, 3)
                shared_up(p, 0)
                transpose_scores(p)
                shared_up(p, 1)
                transpose_pair(p, 0)
                shared_up(p, 2)
                transpose_pair(p, 1)
                for u in range(3, SHARED_UNITS):
                    shared_down(p, u - 3)
                    transpose_pair(p, 2 * u - 4)
                    shared_up(p, u)
                    transpose_pair(p, 2 * u - 3)
                    if u == TRANSPOSE_S_BEHIND:
                        transpose_s(p)
                shared_down(p, SHARED_UNITS - 3)
                for half in range(TOKEN_HALVES):
                    pe.wait_ge(relu_ready, (p + 1) * SHARED_UNITS - 1 + half)
                    expert_up(0, half, p * EXPERTS + 1)
                shared_down(p, SHARED_UNITS - 2)
                shared_down(p, SHARED_UNITS - 1)
                pe.wait_ge(shared_added, (p + 1) * BLOCKS)
                pe.wait_ge(s_t_copied, p + 1)
                up_and_down(p, 0, 0, first=True)
                with pe.Fori(0, EXPERTS // 2 - 1) as i:
                    up_and_down(p, 2 * i, 1)
                    up_and_down(p, 2 * i, 2)
                for half in range(TOKEN_HALVES):
                    expert_down(1, half, (p + 1) * EXPERTS, (p + 1) * UNITS - 2 + half, last_expert=True)
                    if p + 1 < PASSES:
                        project(p + 1, half)
            for q in range(BLOCKS):
                fc2(PASSES - 1, q)

        @block.scalar
        def _(act):
            def round_chunk(c, dst, src):
                act.wait_ge(wt_ready, c + 1)
                act.activation(dst, src, ACT.Copy).then_inc(wt_hi, 1)

            act.wait_ge(const_step, 1)
            act.activation(table_load[:, :], zero[:, :], ACT.Sigmoid).then_inc(table_loaded, 1)
            round_chunk(0, small_hi[:, UP0:DOWN0], h_banks[:, 0, :])
            round_chunk(1, small_hi[:, DOWN0:FC1_0], h_banks[:, 1, :])
            round_chunk(2, small_hi[:, FC1_0:GATE0], y_banks[:, 0, 0:GATE0 - FC1_0])
            act.wait_ge(gate_zeroed, 2)
            act.activation(gate_columns(small_hi), gate_banks, ACT.Copy).then_inc(wt_hi, 1)

            def round_projection(p, b):
                act.wait_ge(xc_ready, p * BLOCKS + b + 1)
                act.activation(xc_hi[:, :, b * BANK:(b + 1) * BANK],
                               h_banks[:, b % 2, :].rearrange("q (a t) -> q a t", a=HALVES), ACT.Copy)\
                    .then_inc(xc_hi_ready, 1)

            def score_and_round_latent(p, b):
                act.wait_ge(logits_ready, p * BLOCKS + b + 1)
                act.activation(scores_t[b * EXPERTS:(b + 1) * EXPERTS, :], y_banks[0:EXPERTS, b % 2, BANK:2 * BANK],
                               ACT.Sigmoid).then_inc(scores_t_ready, 1)
                act.wait_ge(lat_ready, p * BLOCKS + b + 1)
                act.activation(lat_hi[:, b * BANK:(b + 1) * BANK], y_banks[:, b % 2, 0:BANK], ACT.Copy)\
                    .then_inc(lat_hi_ready, 1)

            def copy_experts(n):
                c, w = divmod(n, 2)
                act.wait_ge(experts_transposed, n + 1)
                act.activation(experts_w[:, w, c * W_CHUNK:(c + 1) * W_CHUNK, :].rearrange("q e i -> q (e i)"),
                               y_banks[:, 1, (n % 2) * BANK:(n % 2 + 1) * BANK], ACT.Copy).then_inc(experts_copied, 1)

            def relu_shared(p, u):
                act.wait_ge(h_ready, p * UNITS + u + 1)
                if p > 0 or u >= 2:
                    act.wait_ge(act_full_ready, p * UNITS + u - 1)
                act.activation(scaled[:, u % 2, :], h_banks[:, u % 2, :], ACT.Relu).then_inc(relu_ready, 1)

            def square_shared(p, u):
                act.wait_ge(relu_ready, p * SHARED_UNITS + u + 1)
                if u >= 2:
                    act.wait_ge(down_done, p * SHARED_UNITS + u - 1)
                elif p > 0:
                    act.wait_ge(fc2_done, p * BLOCKS)
                act.activation(act_hi[:, u % 2, :], scaled[:, u % 2, :], ACT.Square).then_inc(act_hi_ready, 1)
                if p > 0 or u >= 2:
                    act.wait_ge(act_lo_ready, p * UNITS + u - 1)
                act.activation(act_full[:, u % 2, :], scaled[:, u % 2, :], ACT.Square).then_inc(act_full_ready, 1)

            def square(p, half, e):
                act.wait_ge(scaled_ready, 2 * e + (p * EXPERT_UNITS + half + 1))
                act.activation(act_hi[:, half, :], scaled[:, half, :], ACT.Square).then_inc(act_hi_ready, 1)
                act.wait_ge(act_lo_ready, 2 * e + (p * UNITS + SHARED_UNITS + half - 1))
                act.activation(act_full[:, half, :], scaled[:, half, :], ACT.Square).then_inc(act_full_ready, 1)

            def round_output(p, half):
                act.wait_ge(experts_done, (p + 1) * EXPERT_UNITS - 1 + half)
                act.activation(act_hi[:, half, :], y_banks[:, half, :], ACT.Copy).then_inc(y_hi_ready, 1)

            def copy_pair(p, k):
                if p == 0 and k < W_CHUNKS:
                    copy_experts(2 * k)
                    copy_experts(2 * k + 1)

            for p in range(PASSES):
                for b in range(BLOCKS):
                    if p > 0 and b < TOKEN_HALVES:
                        round_output(p - 1, b)
                    round_projection(p, b)
                    if p == 0 and b >= 2:
                        score_and_round_latent(p, b - 2)
                for b in range(2 if p == 0 else 0, BLOCKS):
                    score_and_round_latent(p, b)
                relu_shared(p, 0)
                act.wait_ge(scores_transposed, p + 1)
                act.activation(scores.rearrange("q (b j) e -> q b j e", b=BLOCKS),
                               y_banks[:, 1, 0:BANK].rearrange("q (j b e) -> q b j e", j=BT, b=BLOCKS), ACT.Copy)\
                    .then_inc(scores_ready, 1)
                square_shared(p, 0)
                relu_shared(p, 1)
                copy_pair(p, 0)
                square_shared(p, 1)
                relu_shared(p, 2)
                copy_pair(p, 1)
                for u in range(2, SHARED_UNITS - 1):
                    copy_pair(p, 2 * u - 2)
                    square_shared(p, u)
                    if u == ROOT_BEHIND:
                        act.wait_ge(cw_ready, p + 1)
                        act.activation(root, masked, ACT.Sqrt, scale=0.25).then_inc(root_ready, 1)
                    if u == TRANSPOSE_S_BEHIND - 1:
                        act.wait_ge(s_t_ready, p + 1)
                        if p > 0:
                            act.wait_ge(s_stored, p * (BT * DMA))
                        act.activation(s_t[:, :], y_banks[:, 1, BANK:2 * BANK], ACT.Copy).then_inc(s_t_copied, 1)
                    relu_shared(p, u + 1)
                    copy_pair(p, 2 * u - 1)
                square_shared(p, SHARED_UNITS - 1)
                for half in range(TOKEN_HALVES):
                    act.wait_ge(down_done, (p + 1) * SHARED_UNITS - 1 + half)
                    square(p, half, 0)
                with act.Fori(1, EXPERTS) as e:
                    for half in range(TOKEN_HALVES):
                        act.wait_ge(experts_done, 2 * e + (p * EXPERT_UNITS + half - 1))
                        square(p, half, e)
            for half in range(TOKEN_HALVES):
                round_output(PASSES - 1, half)

        @block.vector
        def _(dve):
            def rest_of_chunk(c, dst, src, hi):
                dve.wait_ge(wt_hi, c + 1)
                dve.tensor_tensor(dst, src, hi.bitcast(f32), ALU.subtract).then_inc(wt_lo, 1)

            rest_of_chunk(0, small_lo[:, UP0:DOWN0], h_banks[:, 0, :], small_hi[:, UP0:DOWN0])
            rest_of_chunk(1, small_lo[:, DOWN0:FC1_0], h_banks[:, 1, :], small_hi[:, DOWN0:FC1_0])
            rest_of_chunk(2, small_lo[:, FC1_0:GATE0], y_banks[:, 0, 0:GATE0 - FC1_0], small_hi[:, FC1_0:GATE0])
            dve.wait_ge(gate_zeroed, 2)
            rest_of_chunk(3, gate_columns(small_lo), gate_banks, gate_columns(small_hi))

            def rest_of_projection(p, b):
                dve.wait_ge(xc_hi_ready, p * BLOCKS + b + 1)
                cols = slice(b * BANK, (b + 1) * BANK)
                dve.tensor_tensor(xc_lo[:, :, cols], h_banks[:, b % 2, :].rearrange("q (a t) -> q a t", a=HALVES),
                                  xc_hi[:, :, cols].bitcast(f32), ALU.subtract).then_inc(xc_lo_ready, 1)

            def rest_of_latent(p, b):
                dve.wait_ge(lat_hi_ready, p * BLOCKS + b + 1)
                cols = slice(b * BANK, (b + 1) * BANK)
                dve.tensor_tensor(lat_lo[:, cols], y_banks[:, b % 2, 0:BANK], lat_hi[:, cols].bitcast(f32),
                                  ALU.subtract).then_inc(lat_lo_ready, 1)

            def relu_and_scale(half, scale_slot, loads, unit):
                dve.wait_ge(h_ready, unit + 1)
                dve.wait_ge(scale_loaded[scale_slot], loads * DMA)
                dve.wait_ge(act_full_ready, unit - 1)
                dve.scalar_tensor_tensor(scaled[:, half, :], h_banks[:, half, :], 0.0, scale_ring[:, scale_slot, :],
                                         ALU.max, ALU.mult).then_inc(scaled_ready, 1)

            def rest(slot, unit):
                dve.wait_ge(act_hi_ready, unit + 1)
                dve.wait_ge(act_full_ready, unit + 1)
                dve.tensor_tensor(act_lo[:, slot, :], act_full[:, slot, :], act_hi[:, slot, :].bitcast(f32),
                                  ALU.subtract).then_inc(act_lo_ready, 1)

            def add_shared(p, b):
                dve.wait_ge(down_done, p * SHARED_UNITS + 2 * (b + 1))
                if p > 0:
                    dve.wait_ge(out_stored[b], p * DMA)
                tiles = slice(BT * b, BT * (b + 1))
                dve.tensor_tensor(x_res[:, tiles, :], y_banks[:, 0, :].rearrange("q (j h) -> q j h", h=H),
                                  x_in[:, tiles, :], ALU.add).then_inc(shared_added, 1)

            def rest_of_output(p, half):
                dve.wait_ge(y_hi_ready, p * TOKEN_HALVES + half + 1)
                dve.tensor_tensor(act_lo[:, half, :], y_banks[:, half, :], act_hi[:, half, :].bitcast(f32),
                                  ALU.subtract).then_inc(y_lo_ready, 1)

            def add_routed(p, q):
                dve.wait_ge(fc2_done, p * BLOCKS + q + 1)
                tiles = slice(BT * q, BT * (q + 1))
                dve.tensor_tensor(x_res[:, tiles, :], y_banks[:, q % 2, :].rearrange("q (j h) -> q j h", h=H),
                                  x_res[:, tiles, :], ALU.add).then_inc(routed_added, 1)

            steps = [0]

            def step(instruction):
                instruction.then_inc(gate_step, 1)
                steps[0] += 1

            def steps_done():
                dve.wait_ge(gate_step, steps[0])

            def grouped(t):
                return t[:, :, :].rearrange("q n (g k) -> q (n g) k", g=GROUPS)

            def per_group(t):
                return t[:, :, :].rearrange("q n g -> q (n g)")

            def over_group(t):
                return per_group(t).unsqueeze(2).to_broadcast([P, TILES * GROUPS, GROUP_SIZE])

            def group_scores(p):
                if p == 0:
                    dve.wait_ge(cond_stored, DMA)
                dve.wait_ge(scores_ready, p + 1)
                step(dve.tensor_tensor(biased, scores,
                                       bias_sb[:, :].unsqueeze(1).to_broadcast([P, TILES, EXPERTS]), ALU.add))
                steps_done()
                step(dve.tensor_reduce(per_group(first), grouped(biased), AX.X, ALU.max))
                steps_done()
                rest(0, p * UNITS)
                step(dve.tensor_tensor(grouped(work), grouped(biased), over_group(first), ALU.is_equal))
                steps_done()
                step(dve.tensor_reduce(per_group(count), grouped(work), AX.X, ALU.add))
                step(dve.scalar_tensor_tensor(grouped(left), grouped(work), -BIG, grouped(biased), ALU.mult, ALU.add))
                steps_done()
                step(dve.tensor_reduce(per_group(second), grouped(left), AX.X, ALU.max))
                step(dve.tensor_scalar(per_group(count), per_group(count), 1.5, -BIG, ALU.is_lt, ALU.mult))
                steps_done()
                step(dve.tensor_tensor(per_group(count), per_group(count), per_group(first), ALU.add))
                steps_done()
                step(dve.tensor_tensor(per_group(second), per_group(second), per_group(count), ALU.max))
                steps_done()
                step(dve.tensor_tensor(per_group(group_score), per_group(first), per_group(second), ALU.add))
                steps_done()

            def pick_groups():
                full = [P, TILES, GROUPS, GROUPS]
                other = group_score[:, :, :].unsqueeze(2).to_broadcast(full)
                own = group_score[:, :, :].unsqueeze(3).to_broadcast(full)
                step(dve.tensor_tensor(group_gt[:, :, :, :], other, own, ALU.is_gt))
                step(dve.tensor_tensor(group_eq[:, :, :, :], other, own, ALU.is_equal))
                steps_done()
                step(dve.tensor_tensor(group_eq[:, :, :, :], group_eq[:, :, :, :],
                                       before[:, :, :].unsqueeze(1).to_broadcast(full), ALU.mult))
                steps_done()
                step(dve.tensor_tensor(group_gt[:, :, :, :], group_gt[:, :, :, :], group_eq[:, :, :, :], ALU.add))
                steps_done()
                step(dve.tensor_reduce(per_group(count), group_gt[:, :, :, :].rearrange("q n g k -> q (n g) k"),
                                       AX.X, ALU.add))
                steps_done()
                step(dve.tensor_scalar(per_group(count), per_group(count), TOP_GROUPS - 0.5, -BIG,
                                       ALU.is_gt, ALU.mult))
                steps_done()
                step(dve.tensor_tensor(grouped(masked), grouped(biased), over_group(count), ALU.add))
                steps_done()

            def largest():
                for n in range(TILES):
                    step(dve.max(top8[:, n, :], masked[:, n, :]))

            def mark():
                for n in range(TILES):
                    step(dve.match_replace(left[:, n, :], top8[:, n, :], masked[:, n, :], TAKEN))

            def combine_weights():
                step(dve.scalar_tensor_tensor(work, left, TAKEN, scores,
                                              ALU.is_equal, ALU.mult))
                steps_done()
                step(dve.tensor_reduce(total[:, :], work, AX.X, ALU.add))
                steps_done()
                step(dve.reciprocal(total[:, :], total[:, :]))
                steps_done()
                step(dve.scalar_tensor_tensor(cw, work, ROUTED_SCALE,
                                              total[:, :].unsqueeze(2).to_broadcast([P, TILES, EXPERTS]),
                                              ALU.mult, ALU.mult))
                steps_done()
                dve.tensor_scalar(masked, cw, TINY, None, ALU.max).then_inc(cw_ready, 1)

            def root_of_weights(p):
                dve.wait_ge(root_ready, p + 1)
                step(dve.reciprocal(left, root))
                steps_done()
                step(dve.tensor_tensor(left, left, cw, ALU.mult))
                steps_done()
                step(dve.scalar_tensor_tensor(left, left, 0.25, root, ALU.mult, ALU.add))
                steps_done()
                dve.scalar_tensor_tensor(s_tok, cw, 0.0, left,
                                         ALU.is_gt, ALU.mult).then_inc(s_ready, 1)

            dve.wait_ge(bias_loaded, DMA)
            dve.wait_ge(consts_ready, 2)
            for p in range(PASSES):
                if p == 0:
                    for b in range(BLOCKS):
                        rest_of_projection(p, b)
                        if b >= 2:
                            rest_of_latent(p, b - 2)
                    rest_of_latent(p, 2)
                    rest_of_latent(p, 3)
                else:
                    for half in range(TOKEN_HALVES):
                        rest_of_output(p - 1, half)
                        rest_of_projection(p, half)
                    add_routed(p - 1, 0)
                    add_routed(p - 1, 1)
                    rest_of_projection(p, 2)
                    add_routed(p - 1, 2)
                    rest_of_projection(p, 3)
                    add_routed(p - 1, 3)
                    for b in range(BLOCKS):
                        rest_of_latent(p, b)
                shared = p * UNITS
                group_scores(p)
                rest(1, shared + 1)
                pick_groups()
                largest()
                steps_done()
                mark()
                steps_done()
                if p == 0:
                    combine_weights()
                add_shared(p, 0)
                rest(0, shared + 2)
                if p > 0:
                    combine_weights()
                rest(1, shared + 3)
                root_of_weights(p)
                add_shared(p, 1)
                rest(0, shared + 4)
                rest(1, shared + 5)
                rest(0, shared + 6)
                add_shared(p, 2)
                base = p * UNITS + SHARED_UNITS
                loads = p * (EXPERTS // 2)
                relu_and_scale(0, 0, loads + 1, base)
                rest(1, shared + 7)
                relu_and_scale(1, 1, loads + 1, base + 1)
                add_shared(p, 3)
                with dve.Fori(0, EXPERTS // 2 - 1) as i:
                    for u in range(4):
                        rest(u % 2, 4 * i + (base + u))
                        relu_and_scale(u % 2, (u + 2) % 4, i + (loads + (1 if u < 2 else 2)), 4 * i + (base + u + 2))
                for u in range(EXPERT_UNITS - 4, EXPERT_UNITS):
                    rest(u % 2, base + u)
                    if u + 2 < EXPERT_UNITS:
                        relu_and_scale(u % 2, (u + 2) % 4, loads + EXPERTS // 2, base + u + 2)
            for half in range(TOKEN_HALVES):
                rest_of_output(PASSES - 1, half)
            for q in range(BLOCKS):
                add_routed(PASSES - 1, q)


def kernel(x, itok_B_1_198, L0_cond_weights, L0_ffn_gate_w, L0_ffn_gate_bias, L0_ffn_fc1_w, L0_ffn_fc2_w,
           L0_ffn_w1, L0_ffn_w2, L0_ffn_shared_up_w, L0_ffn_shared_down_w):
    import numpy as np
    import concourse.bacc as bacc
    from concourse.bass_utils import run_bass_kernel_spmd

    given = {"x": x, "cond": itok_B_1_198, "cond_w": L0_cond_weights, "gate_w": L0_ffn_gate_w,
             "gate_b": L0_ffn_gate_bias, "fc1_w": L0_ffn_fc1_w, "fc2_w": L0_ffn_fc2_w, "w1": L0_ffn_w1,
             "w2": L0_ffn_w2, "up_w": L0_ffn_shared_up_w, "down_w": L0_ffn_shared_down_w}
    nc = bacc.Bacc("TRN2", target_bir_lowering=False, num_devices=1)
    arrays, args = {}, {}
    for name, value in given.items():
        a = np.ascontiguousarray(value)
        arrays[f"in_{name}"] = a
        args[name] = nc.dram_tensor(f"in_{name}", a.shape, mybir.dt.from_np(a.dtype), kind="ExternalInput").ap()
    out = nc.dram_tensor("out_x", (B, C, H), mybir.dt.float32, kind="ExternalOutput").ap()
    adaln_ffn(nc, **args, out=out)
    result = run_bass_kernel_spmd(nc, [arrays], core_ids=[0])
    return result.results[0]["out_x"]
```

```python
from contextlib import ExitStack

import concourse.bass as bass
from concourse import mybir

B, C, H = 128, 32, 256
EXPERTS, LAT, INTER = 32, 128, 128
GROUPS, TOP_GROUPS, TOP_K = 4, 2, 8
GROUP_SIZE = EXPERTS // GROUPS
SHARED = 512
ROUTED_SCALE = 2.5
P = 128
TOKENS = B * C
PASSES = 2
PASS_TOKENS = TOKENS // PASSES
BANK = 512
BLOCKS = PASS_TOKENS // BANK
PASS_BATCHES = B // PASSES
TILES = PASS_TOKENS // P
BT = TILES // BLOCKS
BATCH_TILE = P // C
HALVES = H // P
TILES_OF_BANK = BANK // H
UNIT = 2 * BANK
SHARED_CHUNKS = SHARED // P
SHARED_UNITS = BLOCKS * 2
TOKEN_HALVES = PASS_TOKENS // UNIT
EXPERT_UNITS = EXPERTS * TOKEN_HALVES
UNITS = SHARED_UNITS + EXPERT_UNITS
W_CHUNK = 4
W_CHUNKS = EXPERTS // W_CHUNK
SMALL_SPLITS = 4
RAW_EXPERTS = 8
RAW_LOADS = EXPERTS // RAW_EXPERTS
ROOT_BEHIND = 3
TRANSPOSE_S_BEHIND = 6
BIG = 1e38
TAKEN = -3e38
TINY = 1e-30
WARM_UP = 12
DMA = 16

UP0 = 0
DOWN0 = UP0 + HALVES * SHARED
FC1_0 = DOWN0 + SHARED_CHUNKS * H
FC2_0 = FC1_0 + HALVES * LAT
GATE0 = FC2_0 + H
SMALL = GATE0 + HALVES * P


def adaln_ffn(nc, x, cond, cond_w, gate_w, gate_b, fc1_w, fc2_w, w1, w2, up_w, down_w, out):
    f32, f32r, i32 = mybir.dt.float32, mybir.dt.float32r, mybir.dt.int32
    ALU, ACT, AX = mybir.AluOpType, mybir.ActivationFunctionType, mybir.AxisListType

    x_rows = x.rearrange("b c h -> (b c) h").rearrange("(n p) h -> p n h", p=P)
    out_rows = out.rearrange("b c h -> (b c) h").rearrange("(n p) h -> p n h", p=P)

    cond_dram = nc.dram_tensor("cond_dram", (B, C, C), f32).ap()
    s_dram = nc.dram_tensor("s_dram", (EXPERTS, PASS_TOKENS), f32).ap()

    with ExitStack() as ctx:
        def sb(name, shape, dt=f32):
            return ctx.enter_context(nc.sbuf_tensor(name, shape, dt))

        def sem(name):
            return ctx.enter_context(nc.semaphore(name))

        def sems(name, n):
            return [sem(f"{name}{i}") for i in range(n)]

        x_in = sb("x_in", [P, TILES, H])
        x_res = sb("x_res", [P, TILES, H])
        cond_bd = sb("cond_bd", [P, TILES, P])
        cond_sb = sb("cond_sb", [PASS_BATCHES, PASSES], i32)
        xc_hi = sb("xc_hi", [P, HALVES, PASS_TOKENS], f32r)
        xc_lo = sb("xc_lo", [P, HALVES, PASS_TOKENS], f32r)
        lat_hi = sb("lat_hi", [P, PASS_TOKENS], f32r)
        lat_lo = sb("lat_lo", [P, PASS_TOKENS], f32r)
        small_hi = sb("small_hi", [P, SMALL], f32r)
        small_lo = sb("small_lo", [P, SMALL], f32r)
        experts_w = sb("experts_w", [P, 2, EXPERTS, P])
        w1_ring = sb("w1_ring", [P, 2, 2, P], f32r)
        w2_ring = sb("w2_ring", [P, 2, 2, P], f32r)
        scale_ring = sb("scale_ring", [P, 4, UNIT])
        scaled = sb("scaled", [P, 2, UNIT])
        act_full = sb("act_full", [P, 2, UNIT])
        act_hi = sb("act_hi", [P, 2, UNIT], f32r)
        act_lo = sb("act_lo", [P, 2, UNIT], f32r)
        s_t = sb("s_t", [P, BANK])
        ident = sb("ident", [P, P])
        bias_sb = sb("bias_sb", [P, EXPERTS])
        zero = sb("zero", [P, 1])
        table_load = sb("table_load", [P, 1])
        before = sb("before", [P, GROUPS, GROUPS])
        scores, biased, work, masked, left, cw, root, s_tok = (
            scale_ring[:, n // 2, (n % 2) * BANK:(n % 2 + 1) * BANK].rearrange("q (n e) -> q n e", e=EXPERTS)
            for n in range(8))
        top8 = sb("top8", [P, TILES, 8])
        first = sb("first", [P, TILES, GROUPS])
        count = sb("count", [P, TILES, GROUPS])
        second = sb("second", [P, TILES, GROUPS])
        group_score = sb("group_score", [P, TILES, GROUPS])
        group_gt = sb("group_gt", [P, TILES, GROUPS, GROUPS])
        group_eq = sb("group_eq", [P, TILES, GROUPS, GROUPS])
        total = sb("total", [P, TILES])

        raw_up = scaled[:, 0, :].rearrange("p (k h) -> p k h", h=H)
        raw_down = scaled[:, 1, :].rearrange("p (a m) -> p a m", m=SHARED)
        raw_fc1 = act_full[:, 0, 0:H]
        raw_fc2 = act_full[:, 0, H:2 * H].rearrange("p (a l) -> p a l", l=LAT)
        raw_gate = act_full[0:EXPERTS, 0, 2 * H:3 * H]
        scores_t = act_full[:, 1, 0:BANK]
        cond_rows = scale_ring[0:PASS_BATCHES, 2:4, :]

        h_banks = ctx.enter_context(nc.psum_tensor("h_banks", [P, 2, UNIT], f32))
        y_banks = ctx.enter_context(nc.psum_tensor("y_banks", [P, 2, UNIT], f32))

        def per_half(t):
            return t.rearrange("q (a e) -> q a e", a=HALVES)

        def parts(p, q):
            n = 2 if p == PASSES - 1 else 1
            return [(p * BLOCKS + n * q + k + 1, range(k * BT // n, (k + 1) * BT // n)) for k in range(n)]

        def routed_banks(p, q):
            return (h_banks if p == PASSES - 1 and q < 2 else y_banks)[:, q % 2, :]

        gate_banks = per_half(y_banks[:, 0, 2 * H:2 * H + HALVES * EXPERTS])

        def gate_columns(weights):
            return per_half(weights[:, GATE0:SMALL])[:, :, 0:EXPERTS]

        x_loaded = sems("x_loaded", BLOCKS)
        cond_idx_loaded = sems("cond_idx_loaded", PASSES)
        bias_loaded = sem("bias_loaded")
        up_loaded = sem("up_loaded")
        down_loaded = sem("down_loaded")
        small_loaded = sem("small_loaded")
        raw_loaded = sems("raw_loaded", RAW_LOADS)
        cond_gathered = sems("cond_gathered", PASSES)
        cond_stored = sems("cond_stored", PASSES)
        cond_loaded = sem("cond_loaded")
        s_stored = sem("s_stored")
        scale_loaded = sems("scale_loaded", 4)
        out_stored = sems("out_stored", BLOCKS)
        const_step = sem("const_step")
        consts_ready = sem("consts_ready")
        cond_zeroed = sem("cond_zeroed")
        gate_zeroed = sem("gate_zeroed")
        w1_lo = sem("w1_lo")
        w2_lo = sem("w2_lo")
        wt_ready = sem("wt_ready")
        experts_transposed = sem("experts_transposed")
        xc_ready = sem("xc_ready")
        logits_ready = sem("logits_ready")
        lat_ready = sem("lat_ready")
        h_ready = sem("h_ready")
        down_done = sem("down_done")
        scores_transposed = sem("scores_transposed")
        s_t_ready = sem("s_t_ready")
        experts_done = sem("experts_done")
        fc2_done = sem("fc2_done")
        table_loaded = sem("table_loaded")
        wt_hi = sem("wt_hi")
        w1_hi = sem("w1_hi")
        w2_hi = sem("w2_hi")
        experts_copied = sem("experts_copied")
        xc_hi_ready = sem("xc_hi_ready")
        lat_hi_ready = sem("lat_hi_ready")
        scores_t_ready = sem("scores_t_ready")
        scores_ready = sem("scores_ready")
        root_ready = sem("root_ready")
        relu_ready = sem("relu_ready")
        act_hi_ready = sem("act_hi_ready")
        act_full_ready = sem("act_full_ready")
        s_t_copied = sem("s_t_copied")
        y_hi_ready = sem("y_hi_ready")
        wt_lo = sem("wt_lo")
        xc_lo_ready = sem("xc_lo_ready")
        lat_lo_ready = sem("lat_lo_ready")
        gate_step = sem("gate_step")
        cw_ready = sem("cw_ready")
        s_ready = sem("s_ready")
        scaled_ready = sem("scaled_ready")
        act_lo_ready = sem("act_lo_ready")
        shared_added = sem("shared_added")
        y_lo_ready = sem("y_lo_ready")
        routed_added = sem("routed_added")

        block = ctx.enter_context(nc.Block())

        def three(w_hi, w_lo, v_hi, v_lo):
            return ((w_hi, v_hi), (w_lo, v_hi), (w_hi, v_lo))

        @block.sync
        def _(sp):
            for p in range(PASSES):
                sp.dma_start(cond_sb[:, p:p + 1], cond[p * PASS_BATCHES:(p + 1) * PASS_BATCHES]
                             .rearrange("(b a) -> b a", a=1)).then_inc(cond_idx_loaded[p], DMA)
            sp.dma_start(raw_up, up_w.rearrange("(k p) h -> p k h", p=P)).then_inc(up_loaded, DMA)
            sp.dma_start(raw_down, down_w.rearrange("(a p) m -> p a m", p=P)).then_inc(down_loaded, DMA)

            def load_x(p, b):
                sp.dma_start(x_in[:, BT * b:BT * (b + 1), :],
                             x_rows[:, p * TILES + BT * b:p * TILES + BT * (b + 1), :]).then_inc(x_loaded[b], DMA)

            def load_cond(p):
                for j in range(BATCH_TILE):
                    sp.dma_start(
                        cond_bd[C * j:C * (j + 1), :, C * j:C * (j + 1)],
                        cond_dram[p * PASS_BATCHES:(p + 1) * PASS_BATCHES]
                        .rearrange("(g j) c d -> j c g d", j=BATCH_TILE)[j],
                    ).then_inc(cond_loaded, DMA)

            def store_cond(p):
                sp.wait_ge(cond_gathered[p], DMA)
                sp.dma_start(cond_dram[p * PASS_BATCHES:(p + 1) * PASS_BATCHES].rearrange("b c d -> b (c d)"),
                             cond_rows[:, p, :]).then_inc(cond_stored[p], DMA)

            store_cond(0)
            sp.dma_start(raw_fc1, fc1_w).then_inc(small_loaded, DMA)
            sp.dma_start(raw_fc2, fc2_w.rearrange("(a p) l -> p a l", p=P)).then_inc(small_loaded, DMA)
            sp.dma_start(raw_gate, gate_w).then_inc(small_loaded, DMA)
            load_x(0, 0)
            sp.wait_ge(cond_zeroed, 1)
            sp.wait_ge(cond_stored[0], DMA)
            load_cond(0)
            for b in range(1, BLOCKS):
                load_x(0, b)
            for p in range(1, PASSES):
                store_cond(p)
            for c in range(RAW_LOADS):
                experts = slice(c * RAW_EXPERTS, (c + 1) * RAW_EXPERTS)
                for w, src in enumerate((w1, w2)):
                    sp.dma_start(experts_w[:, w, experts, :], src[experts].rearrange("e p i -> p e i"))\
                        .then_inc(raw_loaded[c], DMA)

            def load_scale(slot, e, half):
                src = s_dram[bass.ds(e, 1), half * UNIT:(half + 1) * UNIT]
                sp.dma_start(scale_ring[:, slot, :], src.to_broadcast([P, UNIT]))\
                    .then_inc(scale_loaded[slot], DMA)

            for p in range(PASSES):
                sp.wait_ge(s_t_copied, p + 1)
                for j in range(BT):
                    sp.dma_start(
                        s_dram.rearrange("e (b j t) -> j e b t", b=BLOCKS, j=BT)[j],
                        s_t[EXPERTS * j:EXPERTS * (j + 1), :].rearrange("e (b t) -> e b t", b=BLOCKS),
                    ).then_inc(s_stored, DMA)
                sp.wait_ge(s_stored, (p + 1) * BT * DMA)
                for slot in range(4):
                    load_scale(slot, slot // 2, slot % 2)
                if p + 1 < PASSES:
                    sp.wait_ge(cond_stored[p + 1], DMA)
                    sp.wait_ge(xc_ready, (p + 1) * BLOCKS)
                    load_cond(p + 1)
                    for b in range(BLOCKS):
                        sp.wait_ge(shared_added, p * BLOCKS + b + 1)
                        load_x(p + 1, b)
                with sp.Fori(0, EXPERTS // 2 - 1) as i:
                    for slot in range(4):
                        sp.wait_ge(scaled_ready, 4 * i + (p * EXPERT_UNITS + slot + 1))
                        load_scale(slot, 2 * i + (slot // 2 + 2), slot % 2)
                for q in range(BLOCKS):
                    for count_of_part, tiles in parts(p, q):
                        sp.wait_ge(routed_added, count_of_part)
                        first_tile, end = BT * q + tiles[0], BT * q + tiles[-1] + 1
                        sp.dma_start(out_rows[:, p * TILES + first_tile:p * TILES + end, :],
                                     x_res[:, first_tile:end, :]).then_inc(out_stored[q], DMA)
            for q in range(BLOCKS):
                sp.wait_ge(out_stored[q], sum(len(parts(p, q)) for p in range(PASSES)) * DMA)

        @block.gpsimd
        def _(pool):
            pool.memset(zero[:, :], 0.0).then_inc(const_step, 1)
            pool.memset(ident[:, :], 0.0).then_inc(const_step, 1)
            pool.memset(before[:, :, :], 0.0).then_inc(const_step, 1)
            pool.wait_ge(const_step, 3)
            pool.affine_select(out=ident[:, :], in_=ident[:, :], compare_op=ALU.not_equal, fill=1.0, base=0,
                               pattern=[[-1, P]], channel_multiplier=1).then_inc(consts_ready, 1)
            for p in range(PASSES):
                pool.wait_ge(cond_idx_loaded[p], DMA)
                pool.indirect_dma_start(
                    cond_rows[:, p, :], None, cond_w.rearrange("s c d -> s (c d)"),
                    bass.IndirectOffsetOnAxis(ap=cond_sb[:, p:p + 1], axis=0)).then_inc(cond_gathered[p], DMA)
            pool.dma_start(bias_sb[:, :], gate_b.rearrange("(a e) -> a e", a=1).to_broadcast([P, EXPERTS]))\
                .then_inc(bias_loaded, DMA)
            pool.affine_select(out=before[:, :, :], in_=before[:, :, :], compare_op=ALU.is_ge, fill=1.0, base=0,
                               pattern=[[-1, GROUPS], [1, GROUPS]], channel_multiplier=0).then_inc(consts_ready, 1)
            pool.memset(cond_bd[:, :, :], 0.0).then_inc(cond_zeroed, 1)
            pool.memset(small_hi[:, GATE0:SMALL].bitcast(f32), 0.0).then_inc(gate_zeroed, 1)
            pool.memset(small_lo[:, GATE0:SMALL].bitcast(f32), 0.0).then_inc(gate_zeroed, 1)

            def rest_of_weight(p, w, slot, e):
                ring, hi_ready, lo_ready = ((w1_ring, w1_hi, w1_lo), (w2_ring, w2_hi, w2_lo))[w]
                pool.wait_ge(hi_ready, e + (p * EXPERTS + 1))
                pool.tensor_tensor(ring[:, slot, 1, :], experts_w[:, w, bass.ds(e, 1), :].rearrange("q a i -> q (a i)"),
                                   ring[:, slot, 0, :].bitcast(f32), ALU.subtract).then_inc(lo_ready, 1)

            for p in range(PASSES):
                rest_of_weight(p, 0, 0, 0)
                rest_of_weight(p, 1, 0, 0)
                rest_of_weight(p, 0, 1, 1)
                with pool.Fori(0, EXPERTS // 2 - 1) as i:
                    for k in range(2):
                        rest_of_weight(p, 0, k, 2 * i + (k + 2))
                        rest_of_weight(p, 1, 1 - k, 2 * i + (k + 1))
                rest_of_weight(p, 1, 1, EXPERTS - 1)

        @block.tensor
        def _(pe):
            def transpose_chunk(jobs):
                for dst, src, n in jobs:
                    last = pe.transpose(dst, src, ident[0:n, 0:n])
                last.then_inc(wt_ready, 1)

            def keep_warm(n):
                for _ in range(n):
                    pe.transpose(y_banks[:, 1, 0:P], ident[:, :], ident[:, :])

            pe.wait_ge(consts_ready, 1)
            pe.wait_ge(up_loaded, DMA)
            transpose_chunk([(h_banks[:, 0, a * SHARED + k * P:a * SHARED + (k + 1) * P],
                              raw_up[:, k, a * P:(a + 1) * P], P)
                             for a in range(HALVES) for k in range(SHARED_CHUNKS)])
            pe.wait_ge(down_loaded, DMA)
            transpose_chunk([(h_banks[:, 1, k * H + a * P:k * H + (a + 1) * P],
                              raw_down[:, a, k * P:(k + 1) * P], P)
                             for k in range(SHARED_CHUNKS) for a in range(HALVES)])
            keep_warm(WARM_UP)
            pe.wait_ge(small_loaded, 3 * DMA)
            transpose_chunk([(y_banks[:, 0, a * LAT:(a + 1) * LAT], raw_fc1[:, a * P:(a + 1) * P], P)
                             for a in range(HALVES)]
                            + [(y_banks[:, 0, H + a * P:H + (a + 1) * P], raw_fc2[:, a, :], P)
                               for a in range(HALVES)]
                            + [(y_banks[:, 0, 2 * H + a * EXPERTS:2 * H + (a + 1) * EXPERTS],
                                raw_gate[:, a * P:(a + 1) * P], EXPERTS) for a in range(HALVES)])

            keep_warm(WARM_UP)

            def transpose_experts(n):
                c, w = divmod(n, 2)
                if n % (2 * RAW_EXPERTS // W_CHUNK) == 0:
                    pe.wait_ge(raw_loaded[c * W_CHUNK // RAW_EXPERTS], 2 * DMA)
                if n == 0:
                    pe.wait_ge(scores_ready, 1)
                if n >= 2:
                    pe.wait_ge(experts_copied, n - 1)
                for e in range(W_CHUNK):
                    last = pe.transpose(y_banks[:, 1, (n % 2) * BANK + e * P:(n % 2) * BANK + (e + 1) * P],
                                        experts_w[:, w, c * W_CHUNK + e, :], ident[:, :])
                last.then_inc(experts_transposed, 1)

            def project(p, b):
                pe.wait_ge(x_loaded[b], (p + 1) * DMA)
                pe.wait_ge(cond_loaded, (p + 1) * (BATCH_TILE * DMA))
                if b >= 2:
                    pe.wait_ge(xc_hi_ready, p * BLOCKS + b - 1)
                    pe.wait_ge(xc_lo_ready, p * BLOCKS + b - 1)
                elif p == 0:
                    pe.wait_ge(wt_hi, b + 1)
                    pe.wait_ge(wt_lo, b + 1)
                else:
                    pe.wait_ge(scaled_ready, p * EXPERT_UNITS - 1 + b)
                for a in range(HALVES):
                    for g in range(BT):
                        last = pe.matmul(h_banks[:, b % 2, a * BANK + g * P:a * BANK + (g + 1) * P],
                                         x_in[:, b * BT + g, a * P:(a + 1) * P], cond_bd[:, b * BT + g, :],
                                         start=True, stop=True)
                last.then_inc(xc_ready, 1)

            def gate_and_latent(p, b):
                pe.wait_ge(xc_hi_ready, p * BLOCKS + b + 1)
                pe.wait_ge(xc_lo_ready, p * BLOCKS + b + 1)
                if b >= 2:
                    pe.wait_ge(lat_hi_ready, p * BLOCKS + b - 1)
                    pe.wait_ge(lat_lo_ready, p * BLOCKS + b - 1)
                    pe.wait_ge(scores_t_ready, p * BLOCKS + b - 1)
                elif p == 0:
                    pe.wait_ge(wt_hi, SMALL_SPLITS)
                    pe.wait_ge(wt_lo, SMALL_SPLITS)
                else:
                    pe.wait_ge(routed_added, p * BLOCKS - 1 + b)
                terms = [t for a in range(HALVES) for t in three(
                    *(w[:, GATE0 + a * P:GATE0 + (a + 1) * P] for w in (small_hi, small_lo)),
                    *(v[:, a, b * BANK:(b + 1) * BANK] for v in (xc_hi, xc_lo)))]
                for n, (w, v) in enumerate(terms):
                    last = pe.matmul(y_banks[:, b % 2, BANK:2 * BANK], w, v, start=n == 0, stop=n == len(terms) - 1)
                last.then_inc(logits_ready, 1)
                terms = [t for a in range(HALVES) for t in three(
                    *(w[:, FC1_0 + a * LAT:FC1_0 + (a + 1) * LAT] for w in (small_hi, small_lo)),
                    *(v[:, a, b * BANK:(b + 1) * BANK] for v in (xc_hi, xc_lo)))]
                for n, (w, v) in enumerate(terms):
                    last = pe.matmul(y_banks[:, b % 2, 0:BANK], w, v, start=n == 0, stop=n == len(terms) - 1)
                last.then_inc(lat_ready, 1)

            def shared_up(p, u):
                b = u // 2
                if u < 2:
                    pe.wait_ge(xc_hi_ready, p * BLOCKS + u + 3)
                    pe.wait_ge(xc_lo_ready, p * BLOCKS + u + 3)
                else:
                    pe.wait_ge(relu_ready, p * SHARED_UNITS + u - 1)
                for m in range(2):
                    k = 2 * (u % 2) + m
                    terms = [t for a in range(HALVES) for t in three(
                        *(w[:, UP0 + a * SHARED + k * P:UP0 + a * SHARED + (k + 1) * P] for w in (small_hi, small_lo)),
                        *(v[:, a, b * BANK:(b + 1) * BANK] for v in (xc_hi, xc_lo)))]
                    for n, (w, v) in enumerate(terms):
                        last = pe.matmul(h_banks[:, u % 2, m * BANK:(m + 1) * BANK], w, v,
                                         start=n == 0, stop=n == len(terms) - 1)
                last.then_inc(h_ready, 1)

            def shared_down(p, u):
                b, slot = divmod(u, 2)
                pe.wait_ge(act_hi_ready, p * UNITS + u + 1)
                pe.wait_ge(act_lo_ready, p * UNITS + u + 1)
                if u == 0:
                    pe.wait_ge(lat_hi_ready, p * BLOCKS + 3)
                    pe.wait_ge(lat_lo_ready, p * BLOCKS + 3)
                elif slot == 0:
                    pe.wait_ge(shared_added, p * BLOCKS + b)
                for j in range(BT):
                    terms = []
                    for m in range(2):
                        k = 2 * slot + m
                        cols = slice(m * BANK + j * P, m * BANK + (j + 1) * P)
                        terms += three(act_hi[:, slot, cols], act_lo[:, slot, cols],
                                       *(w[:, DOWN0 + k * H:DOWN0 + (k + 1) * H] for w in (small_hi, small_lo)))
                    for n, (v, w) in enumerate(terms):
                        last = pe.matmul(y_banks[:, 0, j * H:(j + 1) * H], v, w,
                                         start=slot == 0 and j % TILES_OF_BANK == 0 and n == 0,
                                         stop=slot == 1 and j % TILES_OF_BANK == TILES_OF_BANK - 1
                                         and n == len(terms) - 1)
                last.then_inc(down_done, 1)

            def transpose_scores(p):
                pe.wait_ge(lat_hi_ready, (p + 1) * BLOCKS)
                pe.wait_ge(lat_lo_ready, (p + 1) * BLOCKS)
                pe.wait_ge(scores_t_ready, (p + 1) * BLOCKS)
                for j in range(BT):
                    last = pe.transpose(y_banks[:, 1, j * P:(j + 1) * P], scores_t[:, j * P:(j + 1) * P], ident[:, :])
                last.then_inc(scores_transposed, 1)

            def transpose_s(p):
                pe.wait_ge(experts_copied, 2 * W_CHUNKS)
                pe.wait_ge(s_ready, p + 1)
                for b in range(BLOCKS):
                    last = pe.transpose(y_banks[:, 1, BANK + b * P:BANK + (b + 1) * P],
                                        s_tok[:, BT * b:BT * (b + 1), :].rearrange("t j e -> t (j e)"), ident[:, :])
                last.then_inc(s_t_ready, 1)

            def transpose_pair(p, k):
                if p == 0 and k < W_CHUNKS:
                    transpose_experts(2 * k)
                    transpose_experts(2 * k + 1)

            def expert_up(slot, half, split_experts):
                if half == 0:
                    pe.wait_ge(w1_lo, split_experts)
                for m in range(2):
                    cols = slice(half * UNIT + m * BANK, half * UNIT + (m + 1) * BANK)
                    terms = three(w1_ring[:, slot, 0], w1_ring[:, slot, 1], lat_hi[:, cols], lat_lo[:, cols])
                    for n, (w, v) in enumerate(terms):
                        last = pe.matmul(h_banks[:, half, m * BANK:(m + 1) * BANK], w, v, start=n == 0, stop=n == 2)
                last.then_inc(h_ready, 1)

            def expert_down(slot, half, split_experts, unit, first_expert=False, last_expert=False):
                if half == 0:
                    pe.wait_ge(w2_lo, split_experts)
                pe.wait_ge(act_hi_ready, unit + 1)
                terms = three(w2_ring[:, slot, 0], w2_ring[:, slot, 1], act_hi[:, half, :], act_lo[:, half, :])
                for n, (w, v) in enumerate(terms):
                    if n == 2:
                        pe.wait_ge(act_lo_ready, unit + 1)
                    for m in range(2):
                        last = pe.matmul(y_banks[:, half, m * BANK:(m + 1) * BANK], w, v[:, m * BANK:(m + 1) * BANK],
                                         start=first_expert and n == 0, stop=last_expert and n == 2)
                last.then_inc(experts_done, 1)

            def up_and_down(p, e, k, first=False):
                unit = 2 * e + (p * UNITS + SHARED_UNITS + 2 * k)
                for half in range(TOKEN_HALVES):
                    pe.wait_ge(scaled_ready, 2 * e + (p * EXPERT_UNITS + 2 * k + half + 1))
                    expert_up((k + 1) % 2, half, e + (p * EXPERTS + k + 2))
                    if first:
                        pe.wait_ge(shared_added, (p + 1) * BLOCKS)
                        pe.wait_ge(s_t_copied, p + 1)
                    expert_down(k % 2, half, e + (p * EXPERTS + k + 1), unit + half, first_expert=first)

            def fc2(p, q):
                pe.wait_ge(y_hi_ready, p * BLOCKS + q + 1)
                pe.wait_ge(y_lo_ready, p * BLOCKS + q + 1)
                if p == PASSES - 1 and q < 2:
                    pe.wait_ge(scaled_ready, (p + 1) * EXPERT_UNITS - 1 + q)
                else:
                    pe.wait_ge(y_lo_ready, p * BLOCKS + 2 * (q % 2) + 2)
                    if p < PASSES - 1 and q >= 2:
                        pe.wait_ge(routed_added, p * BLOCKS + q - 1)
                for _, tiles in parts(p, q):
                    for j in tiles:
                        cols = slice((q % 2) * BANK + j * P, (q % 2) * BANK + (j + 1) * P)
                        terms = three(act_hi[:, q // 2, cols], act_lo[:, q // 2, cols],
                                      small_hi[:, FC2_0:FC2_0 + H], small_lo[:, FC2_0:FC2_0 + H])
                        for n, (v, w) in enumerate(terms):
                            last = pe.matmul(routed_banks(p, q)[:, j * H:(j + 1) * H], v, w, start=n == 0, stop=n == 2)
                    last.then_inc(fc2_done, 1)

            project(0, 0)
            project(0, 1)
            for p in range(PASSES):
                if p == 0:
                    project(p, 2)
                    gate_and_latent(p, 0)
                    project(p, 3)
                    gate_and_latent(p, 1)
                else:
                    fc2(p - 1, 0)
                    fc2(p - 1, 1)
                    project(p, 2)
                    fc2(p - 1, 2)
                    project(p, 3)
                    fc2(p - 1, 3)
                    gate_and_latent(p, 0)
                    gate_and_latent(p, 1)
                gate_and_latent(p, 2)
                gate_and_latent(p, 3)
                shared_up(p, 0)
                transpose_scores(p)
                shared_up(p, 1)
                transpose_pair(p, 0)
                shared_up(p, 2)
                transpose_pair(p, 1)
                for u in range(3, SHARED_UNITS):
                    shared_down(p, u - 3)
                    transpose_pair(p, 2 * u - 4)
                    shared_up(p, u)
                    transpose_pair(p, 2 * u - 3)
                    if u == TRANSPOSE_S_BEHIND:
                        transpose_s(p)
                shared_down(p, SHARED_UNITS - 3)
                for half in range(TOKEN_HALVES):
                    pe.wait_ge(relu_ready, (p + 1) * SHARED_UNITS - 1 + half)
                    expert_up(0, half, p * EXPERTS + 1)
                shared_down(p, SHARED_UNITS - 2)
                shared_down(p, SHARED_UNITS - 1)
                up_and_down(p, 0, 0, first=True)
                with pe.Fori(0, EXPERTS // 2 - 1) as i:
                    up_and_down(p, 2 * i, 1)
                    up_and_down(p, 2 * i, 2)
                for half in range(TOKEN_HALVES):
                    if p + 1 < PASSES:
                        project(p + 1, half)
                    expert_down(1, half, (p + 1) * EXPERTS, (p + 1) * UNITS - 2 + half, last_expert=True)
            for q in range(BLOCKS):
                fc2(PASSES - 1, q)

        @block.scalar
        def _(act):
            def round_chunk(c, dst, src):
                act.wait_ge(wt_ready, c + 1)
                act.activation(dst, src, ACT.Copy).then_inc(wt_hi, 1)

            act.wait_ge(const_step, 1)
            act.activation(table_load[:, :], zero[:, :], ACT.Sigmoid).then_inc(table_loaded, 1)
            round_chunk(0, small_hi[:, UP0:DOWN0], h_banks[:, 0, :])
            round_chunk(1, small_hi[:, DOWN0:FC1_0], h_banks[:, 1, :])
            round_chunk(2, small_hi[:, FC1_0:GATE0], y_banks[:, 0, 0:GATE0 - FC1_0])
            act.wait_ge(gate_zeroed, 2)
            act.activation(gate_columns(small_hi), gate_banks, ACT.Copy).then_inc(wt_hi, 1)

            def round_projection(p, b):
                act.wait_ge(xc_ready, p * BLOCKS + b + 1)
                act.activation(xc_hi[:, :, b * BANK:(b + 1) * BANK],
                               h_banks[:, b % 2, :].rearrange("q (a t) -> q a t", a=HALVES), ACT.Copy)\
                    .then_inc(xc_hi_ready, 1)

            def score_and_round_latent(p, b):
                act.wait_ge(logits_ready, p * BLOCKS + b + 1)
                act.activation(scores_t[b * EXPERTS:(b + 1) * EXPERTS, :], y_banks[0:EXPERTS, b % 2, BANK:2 * BANK],
                               ACT.Sigmoid).then_inc(scores_t_ready, 1)
                act.wait_ge(lat_ready, p * BLOCKS + b + 1)
                act.activation(lat_hi[:, b * BANK:(b + 1) * BANK], y_banks[:, b % 2, 0:BANK], ACT.Copy)\
                    .then_inc(lat_hi_ready, 1)

            def copy_experts(n):
                c, w = divmod(n, 2)
                act.wait_ge(experts_transposed, n + 1)
                act.activation(experts_w[:, w, c * W_CHUNK:(c + 1) * W_CHUNK, :].rearrange("q e i -> q (e i)"),
                               y_banks[:, 1, (n % 2) * BANK:(n % 2 + 1) * BANK], ACT.Copy).then_inc(experts_copied, 1)

            def relu_shared(p, u):
                act.wait_ge(h_ready, p * UNITS + u + 1)
                if p > 0 or u >= 2:
                    act.wait_ge(act_full_ready, p * UNITS + u - 1)
                act.activation(scaled[:, u % 2, :], h_banks[:, u % 2, :], ACT.Relu).then_inc(relu_ready, 1)

            def square_shared(p, u):
                act.wait_ge(relu_ready, p * SHARED_UNITS + u + 1)
                if u >= 2:
                    act.wait_ge(down_done, p * SHARED_UNITS + u - 1)
                elif p > 0:
                    act.wait_ge(fc2_done, p * BLOCKS)
                act.activation(act_hi[:, u % 2, :], scaled[:, u % 2, :], ACT.Square).then_inc(act_hi_ready, 1)
                if p > 0 or u >= 2:
                    act.wait_ge(act_lo_ready, p * UNITS + u - 1)
                act.activation(act_full[:, u % 2, :], scaled[:, u % 2, :], ACT.Square).then_inc(act_full_ready, 1)

            def square(p, half, e):
                act.wait_ge(scaled_ready, 2 * e + (p * EXPERT_UNITS + half + 1))
                act.activation(act_hi[:, half, :], scaled[:, half, :], ACT.Square).then_inc(act_hi_ready, 1)
                act.wait_ge(act_lo_ready, 2 * e + (p * UNITS + SHARED_UNITS + half - 1))
                act.activation(act_full[:, half, :], scaled[:, half, :], ACT.Square).then_inc(act_full_ready, 1)

            def square_expert(p, e):
                for half in range(TOKEN_HALVES):
                    act.wait_ge(experts_done, 2 * e + (p * EXPERT_UNITS + half - 1))
                    square(p, half, e)

            def round_output(p, q):
                act.wait_ge(experts_done, (p + 1) * EXPERT_UNITS - 1 + q // 2)
                cols = slice((q % 2) * BANK, (q % 2 + 1) * BANK)
                act.activation(act_hi[:, q // 2, cols], y_banks[:, q // 2, cols], ACT.Copy).then_inc(y_hi_ready, 1)

            def round_weight(w, slot, e):
                ring, ready = ((w1_ring, w1_hi), (w2_ring, w2_hi))[w]
                act.activation(ring[:, slot, 0, :], experts_w[:, w, bass.ds(e, 1), :].rearrange("q a i -> q (a i)"),
                               ACT.Copy).then_inc(ready, 1)

            def copy_pair(p, k):
                if p == 0 and k < W_CHUNKS:
                    copy_experts(2 * k)
                    copy_experts(2 * k + 1)

            for p in range(PASSES):
                for b in range(BLOCKS):
                    if p > 0 and b in (0, 1):
                        round_projection(p, b)
                        round_output(p - 1, 2 * b)
                        round_output(p - 1, 2 * b + 1)
                    else:
                        round_projection(p, b)
                    if p == 0 and b >= 2:
                        score_and_round_latent(p, b - 2)
                for b in range(2 if p == 0 else 0, BLOCKS):
                    score_and_round_latent(p, b)
                relu_shared(p, 0)
                act.wait_ge(scores_transposed, p + 1)
                act.activation(scores.rearrange("q (b j) e -> q b j e", b=BLOCKS),
                               y_banks[:, 1, 0:BANK].rearrange("q (j b e) -> q b j e", j=BT, b=BLOCKS), ACT.Copy)\
                    .then_inc(scores_ready, 1)
                square_shared(p, 0)
                relu_shared(p, 1)
                copy_pair(p, 0)
                square_shared(p, 1)
                relu_shared(p, 2)
                copy_pair(p, 1)
                for u in range(2, SHARED_UNITS - 1):
                    copy_pair(p, 2 * u - 2)
                    square_shared(p, u)
                    if u == ROOT_BEHIND:
                        act.wait_ge(cw_ready, p + 1)
                        act.activation(root, masked, ACT.Sqrt, scale=0.25).then_inc(root_ready, 1)
                    if u == TRANSPOSE_S_BEHIND - 1:
                        act.wait_ge(s_t_ready, p + 1)
                        if p > 0:
                            act.wait_ge(s_stored, p * (BT * DMA))
                        act.activation(s_t[:, :], y_banks[:, 1, BANK:2 * BANK], ACT.Copy).then_inc(s_t_copied, 1)
                    relu_shared(p, u + 1)
                    copy_pair(p, 2 * u - 1)
                    if u == SHARED_UNITS - 3:
                        act.wait_ge(experts_copied, 2 * W_CHUNKS)
                        if p > 0:
                            act.wait_ge(experts_done, p * EXPERT_UNITS)
                        round_weight(0, 0, 0)
                        round_weight(1, 0, 0)
                        round_weight(0, 1, 1)
                square_shared(p, SHARED_UNITS - 1)
                for half in range(TOKEN_HALVES):
                    act.wait_ge(down_done, (p + 1) * SHARED_UNITS - 1 + half)
                    square(p, half, 0)
                round_weight(0, 0, 2)
                round_weight(1, 1, 1)

                with act.Fori(0, EXPERTS // 2 - 2) as i:
                    for k in (1, 2):
                        square_expert(p, 2 * i + k)
                        round_weight(0, k % 2, 2 * i + (k + 2))
                        round_weight(1, (k + 1) % 2, 2 * i + (k + 1))
                square_expert(p, EXPERTS - 3)
                round_weight(0, 1, EXPERTS - 1)
                round_weight(1, 0, EXPERTS - 2)
                square_expert(p, EXPERTS - 2)
                round_weight(1, 1, EXPERTS - 1)
                square_expert(p, EXPERTS - 1)
            for q in range(BLOCKS):
                round_output(PASSES - 1, q)

        @block.vector
        def _(dve):
            def rest_of_chunk(c, dst, src, hi):
                dve.wait_ge(wt_hi, c + 1)
                dve.tensor_tensor(dst, src, hi.bitcast(f32), ALU.subtract).then_inc(wt_lo, 1)

            rest_of_chunk(0, small_lo[:, UP0:DOWN0], h_banks[:, 0, :], small_hi[:, UP0:DOWN0])
            rest_of_chunk(1, small_lo[:, DOWN0:FC1_0], h_banks[:, 1, :], small_hi[:, DOWN0:FC1_0])
            rest_of_chunk(2, small_lo[:, FC1_0:GATE0], y_banks[:, 0, 0:GATE0 - FC1_0], small_hi[:, FC1_0:GATE0])
            dve.wait_ge(gate_zeroed, 2)
            rest_of_chunk(3, gate_columns(small_lo), gate_banks, gate_columns(small_hi))

            def rest_of_projection(p, b):
                dve.wait_ge(xc_hi_ready, p * BLOCKS + b + 1)
                cols = slice(b * BANK, (b + 1) * BANK)
                dve.tensor_tensor(xc_lo[:, :, cols], h_banks[:, b % 2, :].rearrange("q (a t) -> q a t", a=HALVES),
                                  xc_hi[:, :, cols].bitcast(f32), ALU.subtract).then_inc(xc_lo_ready, 1)

            def rest_of_latent(p, b):
                dve.wait_ge(lat_hi_ready, p * BLOCKS + b + 1)
                cols = slice(b * BANK, (b + 1) * BANK)
                dve.tensor_tensor(lat_lo[:, cols], y_banks[:, b % 2, 0:BANK], lat_hi[:, cols].bitcast(f32),
                                  ALU.subtract).then_inc(lat_lo_ready, 1)

            def relu_and_scale(half, scale_slot, loads, unit):
                dve.wait_ge(h_ready, unit + 1)
                dve.wait_ge(scale_loaded[scale_slot], loads * DMA)
                dve.wait_ge(act_full_ready, unit - 1)
                dve.scalar_tensor_tensor(scaled[:, half, :], h_banks[:, half, :], 0.0, scale_ring[:, scale_slot, :],
                                         ALU.max, ALU.mult).then_inc(scaled_ready, 1)

            def rest(slot, unit):
                dve.wait_ge(act_hi_ready, unit + 1)
                dve.wait_ge(act_full_ready, unit + 1)
                dve.tensor_tensor(act_lo[:, slot, :], act_full[:, slot, :], act_hi[:, slot, :].bitcast(f32),
                                  ALU.subtract).then_inc(act_lo_ready, 1)

            def add_shared(p, b):
                dve.wait_ge(down_done, p * SHARED_UNITS + 2 * (b + 1))
                if p > 0:
                    dve.wait_ge(out_stored[b], p * DMA)
                tiles = slice(BT * b, BT * (b + 1))
                dve.tensor_tensor(x_res[:, tiles, :], y_banks[:, 0, :].rearrange("q (j h) -> q j h", h=H),
                                  x_in[:, tiles, :], ALU.add).then_inc(shared_added, 1)

            def rest_of_output(p, q):
                dve.wait_ge(y_hi_ready, p * BLOCKS + q + 1)
                cols = slice((q % 2) * BANK, (q % 2 + 1) * BANK)
                dve.tensor_tensor(act_lo[:, q // 2, cols], y_banks[:, q // 2, cols],
                                  act_hi[:, q // 2, cols].bitcast(f32), ALU.subtract).then_inc(y_lo_ready, 1)

            def add_routed(p, q):
                for count_of_part, tiles in parts(p, q):
                    dve.wait_ge(fc2_done, count_of_part)
                    banks = routed_banks(p, q)[:, tiles[0] * H:(tiles[-1] + 1) * H].rearrange("q (j h) -> q j h", h=H)
                    sums = x_res[:, BT * q + tiles[0]:BT * q + tiles[-1] + 1, :]
                    dve.tensor_tensor(sums, banks, sums, ALU.add).then_inc(routed_added, 1)

            steps = [0]

            def step(instruction):
                instruction.then_inc(gate_step, 1)
                steps[0] += 1

            def steps_done():
                dve.wait_ge(gate_step, steps[0])

            def grouped(t):
                return t[:, :, :].rearrange("q n (g k) -> q (n g) k", g=GROUPS)

            def per_group(t):
                return t[:, :, :].rearrange("q n g -> q (n g)")

            def over_group(t):
                return per_group(t).unsqueeze(2).to_broadcast([P, TILES * GROUPS, GROUP_SIZE])

            def group_scores(p):
                if p == 0:
                    for stored in cond_stored:
                        dve.wait_ge(stored, DMA)
                dve.wait_ge(scores_ready, p + 1)
                step(dve.tensor_tensor(biased, scores,
                                       bias_sb[:, :].unsqueeze(1).to_broadcast([P, TILES, EXPERTS]), ALU.add))
                steps_done()
                step(dve.tensor_reduce(per_group(first), grouped(biased), AX.X, ALU.max))
                steps_done()
                rest(0, p * UNITS)
                step(dve.tensor_tensor(grouped(work), grouped(biased), over_group(first), ALU.is_equal))
                steps_done()
                step(dve.tensor_reduce(per_group(count), grouped(work), AX.X, ALU.add))
                step(dve.scalar_tensor_tensor(grouped(left), grouped(work), -BIG, grouped(biased), ALU.mult, ALU.add))
                steps_done()
                step(dve.tensor_reduce(per_group(second), grouped(left), AX.X, ALU.max))
                step(dve.tensor_scalar(per_group(count), per_group(count), 1.5, -BIG, ALU.is_lt, ALU.mult))
                steps_done()
                step(dve.tensor_tensor(per_group(count), per_group(count), per_group(first), ALU.add))
                steps_done()
                step(dve.tensor_tensor(per_group(second), per_group(second), per_group(count), ALU.max))
                steps_done()
                step(dve.tensor_tensor(per_group(group_score), per_group(first), per_group(second), ALU.add))
                steps_done()

            def pick_groups():
                full = [P, TILES, GROUPS, GROUPS]
                other = group_score[:, :, :].unsqueeze(2).to_broadcast(full)
                own = group_score[:, :, :].unsqueeze(3).to_broadcast(full)
                step(dve.tensor_tensor(group_gt[:, :, :, :], other, own, ALU.is_gt))
                step(dve.tensor_tensor(group_eq[:, :, :, :], other, own, ALU.is_equal))
                steps_done()
                step(dve.tensor_tensor(group_eq[:, :, :, :], group_eq[:, :, :, :],
                                       before[:, :, :].unsqueeze(1).to_broadcast(full), ALU.mult))
                steps_done()
                step(dve.tensor_tensor(group_gt[:, :, :, :], group_gt[:, :, :, :], group_eq[:, :, :, :], ALU.add))
                steps_done()
                step(dve.tensor_reduce(per_group(count), group_gt[:, :, :, :].rearrange("q n g k -> q (n g) k"),
                                       AX.X, ALU.add))
                steps_done()
                step(dve.tensor_scalar(per_group(count), per_group(count), TOP_GROUPS - 0.5, -BIG,
                                       ALU.is_gt, ALU.mult))
                steps_done()
                step(dve.tensor_tensor(grouped(masked), grouped(biased), over_group(count), ALU.add))
                steps_done()

            def largest():
                for n in range(TILES):
                    step(dve.max(top8[:, n, :], masked[:, n, :]))

            def mark():
                for n in range(TILES):
                    step(dve.match_replace(left[:, n, :], top8[:, n, :], masked[:, n, :], TAKEN))

            def combine_weights():
                step(dve.scalar_tensor_tensor(work, left, TAKEN, scores,
                                              ALU.is_equal, ALU.mult))
                steps_done()
                step(dve.tensor_reduce(total[:, :], work, AX.X, ALU.add))
                steps_done()
                step(dve.reciprocal(total[:, :], total[:, :]))
                steps_done()
                step(dve.scalar_tensor_tensor(cw, work, ROUTED_SCALE,
                                              total[:, :].unsqueeze(2).to_broadcast([P, TILES, EXPERTS]),
                                              ALU.mult, ALU.mult))
                steps_done()
                dve.tensor_scalar(masked, cw, TINY, None, ALU.max).then_inc(cw_ready, 1)

            def root_of_weights(p):
                dve.wait_ge(root_ready, p + 1)
                step(dve.reciprocal(left, root))
                steps_done()
                step(dve.tensor_tensor(left, left, cw, ALU.mult))
                steps_done()
                step(dve.scalar_tensor_tensor(left, left, 0.25, root, ALU.mult, ALU.add))
                steps_done()
                dve.scalar_tensor_tensor(s_tok, cw, 0.0, left,
                                         ALU.is_gt, ALU.mult).then_inc(s_ready, 1)

            dve.wait_ge(bias_loaded, DMA)
            dve.wait_ge(consts_ready, 2)
            for p in range(PASSES):
                if p == 0:
                    for b in range(BLOCKS):
                        rest_of_projection(p, b)
                        if b >= 2:
                            rest_of_latent(p, b - 2)
                    rest_of_latent(p, 2)
                    rest_of_latent(p, 3)
                else:
                    for half in range(TOKEN_HALVES):
                        rest_of_projection(p, half)
                        rest_of_output(p - 1, 2 * half)
                        rest_of_output(p - 1, 2 * half + 1)
                    add_routed(p - 1, 0)
                    add_routed(p - 1, 1)
                    rest_of_projection(p, 2)
                    add_routed(p - 1, 2)
                    rest_of_projection(p, 3)
                    add_routed(p - 1, 3)
                    for b in range(BLOCKS):
                        rest_of_latent(p, b)
                shared = p * UNITS
                group_scores(p)
                rest(1, shared + 1)
                pick_groups()
                largest()
                steps_done()
                mark()
                add_shared(p, 0)
                rest(0, shared + 2)
                steps_done()
                combine_weights()
                rest(1, shared + 3)
                root_of_weights(p)
                add_shared(p, 1)
                rest(0, shared + 4)
                rest(1, shared + 5)
                rest(0, shared + 6)
                add_shared(p, 2)
                base = p * UNITS + SHARED_UNITS
                loads = p * (EXPERTS // 2)
                relu_and_scale(0, 0, loads + 1, base)
                rest(1, shared + 7)
                relu_and_scale(1, 1, loads + 1, base + 1)
                add_shared(p, 3)
                with dve.Fori(0, EXPERTS // 2 - 1) as i:
                    for u in range(4):
                        rest(u % 2, 4 * i + (base + u))
                        relu_and_scale(u % 2, (u + 2) % 4, i + (loads + (1 if u < 2 else 2)), 4 * i + (base + u + 2))
                for u in range(EXPERT_UNITS - 4, EXPERT_UNITS):
                    rest(u % 2, base + u)
                    if u + 2 < EXPERT_UNITS:
                        relu_and_scale(u % 2, (u + 2) % 4, loads + EXPERTS // 2, base + u + 2)
            for q in range(BLOCKS):
                rest_of_output(PASSES - 1, q)
            for q in range(BLOCKS):
                add_routed(PASSES - 1, q)


def kernel(x, itok_B_1_198, L0_cond_weights, L0_ffn_gate_w, L0_ffn_gate_bias, L0_ffn_fc1_w, L0_ffn_fc2_w,
           L0_ffn_w1, L0_ffn_w2, L0_ffn_shared_up_w, L0_ffn_shared_down_w):
    import numpy as np
    import concourse.bacc as bacc
    from concourse.bass_utils import run_bass_kernel_spmd

    given = {"x": x, "cond": itok_B_1_198, "cond_w": L0_cond_weights, "gate_w": L0_ffn_gate_w,
             "gate_b": L0_ffn_gate_bias, "fc1_w": L0_ffn_fc1_w, "fc2_w": L0_ffn_fc2_w, "w1": L0_ffn_w1,
             "w2": L0_ffn_w2, "up_w": L0_ffn_shared_up_w, "down_w": L0_ffn_shared_down_w}
    nc = bacc.Bacc("TRN2", target_bir_lowering=False, num_devices=1)
    arrays, args = {}, {}
    for name, value in given.items():
        a = np.ascontiguousarray(value)
        arrays[f"in_{name}"] = a
        args[name] = nc.dram_tensor(f"in_{name}", a.shape, mybir.dt.from_np(a.dtype), kind="ExternalInput").ap()
    out = nc.dram_tensor("out_x", (B, C, H), mybir.dt.float32, kind="ExternalOutput").ap()
    adaln_ffn(nc, **args, out=out)
    result = run_bass_kernel_spmd(nc, [arrays], core_ids=[0])
    return result.results[0]["out_x"]
```
